# Optimizing a Trainium2 kernel written in Bass

```python
import numpy as np
import jax
import jax.numpy as jnp

def _softmax(x, axis=-1):
    return jax.nn.softmax(x, axis=axis)

def _gelu(x):
    return jax.nn.gelu(x, approximate=True)

def _silu(x):
    return jax.nn.silu(x)

def _sigmoid(x):
    return jax.nn.sigmoid(x)

def _layernorm(x, axis=-1, eps=1e-05):
    m = jnp.mean(x, axis=axis, keepdims=True)
    v = jnp.var(x, axis=axis, keepdims=True)
    return (x - m) / jnp.sqrt(v + eps)

def _scatter_add(tgt, idx, src, axis=0):
    return tgt.at[idx].add(src)

def _segment_sum(src, seg, n):
    return jax.ops.segment_sum(src, seg, n)
kernel_name = 'mk_gnn_resnorm_d2_gnn_r32_b491e4'

def setup_inputs(seed: int=0):
    np.random.seed(seed)
    _w = jnp.asarray

    def _rec_inputs():
        import jax
        import jax.numpy as jnp
        _gk = jax.random.key(seed)
        x = -0.0009044 + 1 * jax.random.normal(jax.random.fold_in(_gk, 1), (3125, 16), jnp.float32)
        src = jax.random.randint(jax.random.fold_in(_gk, 2), (100000,), 0, 3125, jnp.int32)
        dst = jnp.minimum((3125 * jax.random.uniform(jax.random.fold_in(_gk, 3), (100000,)) ** 2.0).astype(jnp.int32), 99999)
        _o = jnp.argsort(dst, stable=True)
        src = src[_o]
        dst = dst[_o]
        edge_attr_16 = 0.000268479 + 0.999861 * jax.random.normal(jax.random.fold_in(_gk, 11), (100000, 16), jnp.float32)
        edge_attr_8 = -5.3897e-05 + 0.999841 * jax.random.normal(jax.random.fold_in(_gk, 12), (100000, 8), jnp.float32)
        node_vec1 = -0.00472126 + 0.997171 * jax.random.normal(jax.random.fold_in(_gk, 14), (3125, 1), jnp.float32)
        return (x, src, dst, edge_attr_16, edge_attr_8, node_vec1)
    x, src, dst, edge_attr_16, edge_attr_8, node_vec1 = _rec_inputs()

    def _L0_gnn_setup():
        import jax, jax.numpy as jnp
        import numpy as np
        N_NODES = 3125
        N_EDGES = 100000
        D_NODE = 16
        D_EDGE = 8
        D_HIDDEN = 16
        key = jax.random.key(seed)
        ks = jax.random.split(key, 8)
        node_features = jax.random.normal(ks[0], (N_NODES, D_NODE), dtype=jnp.float32)
        edge_attr_e3nn = jax.random.normal(ks[1], (N_EDGES, D_EDGE), dtype=jnp.float32)
        node_attr_scalar_raw = jax.random.normal(ks[2], (N_NODES, 1), dtype=jnp.float32)
        W_msg_tp = jax.random.normal(ks[3], (D_NODE, D_EDGE, D_HIDDEN), dtype=jnp.float32)
        W_msg_lin = jax.random.normal(ks[4], (D_HIDDEN, D_HIDDEN), dtype=jnp.float32)
        W_upd_tp = jax.random.normal(ks[5], (D_NODE, D_HIDDEN, D_HIDDEN), dtype=jnp.float32)
        W_upd_lin = jax.random.normal(ks[6], (D_HIDDEN, D_NODE), dtype=jnp.float32)
        edge_index = jax.random.randint(ks[7], (2, N_EDGES), 0, N_NODES, dtype=jnp.int64)
        return {'node_features': node_features, 'edge_attr_e3nn': edge_attr_e3nn, 'node_attr_scalar_raw': node_attr_scalar_raw, 'W_msg_tp': W_msg_tp, 'W_msg_lin': W_msg_lin, 'W_upd_tp': W_upd_tp, 'W_upd_lin': W_upd_lin, 'edge_index': edge_index}
    _L0_gnn_all = _L0_gnn_setup()
    _L0_gnn_in = {k: v for k, v in _L0_gnn_all.items() if k in ('W_msg_tp', 'W_msg_lin', 'W_upd_tp', 'W_upd_lin')}
    del _L0_gnn_all

    def _L1_gnn_setup():
        import jax, jax.numpy as jnp
        import numpy as np
        N_NODES = 625
        N_EDGES = 20000
        F = 16

        def _nnconv(x, src, dst, edge_attr, Wn, bn, Wr, b, n_nodes):
            E = edge_attr.shape[0]
            f_in = x.shape[-1]
            f_out = Wr.shape[-1]
            w = jax.nn.relu(edge_attr @ Wn + bn).reshape(E, f_in, f_out)
            msg = jnp.einsum('ei,eio->eo', x[src], w)
            sums = jax.ops.segment_sum(msg, dst, num_segments=n_nodes)
            cnt = jax.ops.segment_sum(jnp.ones((E,), dtype=x.dtype), dst, num_segments=n_nodes)
            aggr = sums / jnp.maximum(cnt, 1.0)[:, None]
            return aggr + x @ Wr + b
        key = jax.random.key(seed)
        ks = jax.random.split(key, 12)
        s_nn = 1.0 / np.sqrt(F)
        s_r = 1.0 / np.sqrt(F)
        inp = {'x': jax.random.normal(ks[0], (N_NODES, F), dtype=jnp.float32), 'edge_index': jax.random.randint(ks[1], (2, N_EDGES), 0, N_NODES, dtype=jnp.int32), 'edge_attr': jax.random.normal(ks[2], (N_EDGES, F), dtype=jnp.float32)}
        for l, (kw, kr) in enumerate(zip(ks[3:6], ks[6:9]), start=1):
            inp[f'Wn{l}'] = jax.random.normal(kw, (F, F * F), dtype=jnp.float32) * s_nn
            inp[f'bn{l}'] = jnp.zeros((F * F,), dtype=jnp.float32)
            inp[f'Wr{l}'] = jax.random.normal(kr, (F, F), dtype=jnp.float32) * s_r
            inp[f'b{l}'] = jnp.zeros((F,), dtype=jnp.float32)
        return inp
    _L1_gnn_all = _L1_gnn_setup()
    _L1_gnn_in = {k: v for k, v in _L1_gnn_all.items() if k in ('Wn1', 'bn1', 'Wr1', 'b1', 'Wn2', 'bn2', 'Wr2', 'b2', 'Wn3', 'bn3', 'Wr3', 'b3')}
    del _L1_gnn_all
    return {'x': x, 'src': src, 'dst': dst, 'edge_attr_16': edge_attr_16, 'edge_attr_8': edge_attr_8, 'node_vec1': node_vec1, 'L0_gnn_W_msg_tp': _L0_gnn_in['W_msg_tp'], 'L0_gnn_W_msg_lin': _L0_gnn_in['W_msg_lin'], 'L0_gnn_W_upd_tp': _L0_gnn_in['W_upd_tp'], 'L0_gnn_W_upd_lin': _L0_gnn_in['W_upd_lin'], 'L1_gnn_Wn1': _L1_gnn_in['Wn1'], 'L1_gnn_bn1': _L1_gnn_in['bn1'], 'L1_gnn_Wr1': _L1_gnn_in['Wr1'], 'L1_gnn_b1': _L1_gnn_in['b1'], 'L1_gnn_Wn2': _L1_gnn_in['Wn2'], 'L1_gnn_bn2': _L1_gnn_in['bn2'], 'L1_gnn_Wr2': _L1_gnn_in['Wr2'], 'L1_gnn_b2': _L1_gnn_in['b2'], 'L1_gnn_Wn3': _L1_gnn_in['Wn3'], 'L1_gnn_bn3': _L1_gnn_in['bn3'], 'L1_gnn_Wr3': _L1_gnn_in['Wr3'], 'L1_gnn_b3': _L1_gnn_in['b3']}

def reference(x, src, dst, edge_attr_16, edge_attr_8, node_vec1, L0_gnn_W_msg_tp, L0_gnn_W_msg_lin, L0_gnn_W_upd_tp, L0_gnn_W_upd_lin, L1_gnn_Wn1, L1_gnn_bn1, L1_gnn_Wr1, L1_gnn_b1, L1_gnn_Wn2, L1_gnn_bn2, L1_gnn_Wr2, L1_gnn_b2, L1_gnn_Wn3, L1_gnn_bn3, L1_gnn_Wr3, L1_gnn_b3):
    import jax
    import jax.numpy as jnp

    def _L0_gnn_ref(node_features, edge_attr_e3nn, node_attr_scalar_raw, W_msg_tp, W_msg_lin, W_upd_tp, W_upd_lin, edge_index):
        import jax, jax.numpy as jnp
        import numpy as np
        N_NODES = 3125
        N_EDGES = 100000
        D_NODE = 16
        D_EDGE = 8
        D_HIDDEN = 16
        n_nodes = node_features.shape[0]
        row = edge_index[0]
        col = edge_index[1]
        norm_msg_tp = 1.0 / np.float32(np.sqrt(D_NODE * D_EDGE))
        norm_upd_tp = 1.0 / np.float32(np.sqrt(D_NODE * D_HIDDEN))
        norm_lin = 1.0 / np.float32(np.sqrt(D_HIDDEN))
        x_j = node_features[col]
        m = jnp.einsum('ei,ej,ijh->eh', x_j, edge_attr_e3nn, W_msg_tp) * norm_msg_tp
        m = jax.nn.silu(m)
        m = m @ W_msg_lin * norm_lin
        agg = jax.ops.segment_sum(m, row, num_segments=n_nodes)
        u = jnp.einsum('ni,nh,ihk->nk', node_features, agg, W_upd_tp) * norm_upd_tp
        u = jax.nn.silu(u)
        u = u @ W_upd_lin * norm_lin
        return node_features + u

    def _L1_gnn_ref(x, edge_index, edge_attr, Wn1, bn1, Wr1, b1, Wn2, bn2, Wr2, b2, Wn3, bn3, Wr3, b3):
        import jax, jax.numpy as jnp
        import numpy as np
        N_NODES = 625
        N_EDGES = 20000
        F = 16

        def _nnconv(x, src, dst, edge_attr, Wn, bn, Wr, b, n_nodes):
            E = edge_attr.shape[0]
            f_in = x.shape[-1]
            f_out = Wr.shape[-1]
            w = jax.nn.relu(edge_attr @ Wn + bn).reshape(E, f_in, f_out)
            msg = jnp.einsum('ei,eio->eo', x[src], w)
            sums = jax.ops.segment_sum(msg, dst, num_segments=n_nodes)
            cnt = jax.ops.segment_sum(jnp.ones((E,), dtype=x.dtype), dst, num_segments=n_nodes)
            aggr = sums / jnp.maximum(cnt, 1.0)[:, None]
            return aggr + x @ Wr + b
        src, dst = (edge_index[0], edge_index[1])
        n = x.shape[0]
        h = _nnconv(x, src, dst, edge_attr, Wn1, bn1, Wr1, b1, n)
        h = _nnconv(h, src, dst, edge_attr, Wn2, bn2, Wr2, b2, n)
        h = _nnconv(h, src, dst, edge_attr, Wn3, bn3, Wr3, b3, n)
        return h
    edge_index = jnp.stack([src, dst])
    x = _layernorm(x + _L0_gnn_ref(x, edge_attr_8, node_vec1, L0_gnn_W_msg_tp, L0_gnn_W_msg_lin, L0_gnn_W_upd_tp, L0_gnn_W_upd_lin, edge_index), axis=-1)
    x = _layernorm(x + _L1_gnn_ref(x, edge_index, edge_attr_16, L1_gnn_Wn1, L1_gnn_bn1, L1_gnn_Wr1, L1_gnn_b1, L1_gnn_Wn2, L1_gnn_bn2, L1_gnn_Wr2, L1_gnn_b2, L1_gnn_Wn3, L1_gnn_bn3, L1_gnn_Wr3, L1_gnn_b3), axis=-1)
    return x

_drawn_inputs = setup_inputs


def setup_inputs(seed=0):
    import zlib

    import numpy as np

    out = dict(_drawn_inputs(seed))
    spreads = {'L1_gnn_bn1': (0.0, 0.1),
     'L1_gnn_b1': (0.0, 0.1),
     'L1_gnn_bn2': (0.0, 0.1),
     'L1_gnn_b2': (0.0, 0.1),
     'L1_gnn_bn3': (0.0, 0.1),
     'L1_gnn_b3': (0.0, 0.1)}
    factors = {}
    for name, (base, spread) in spreads.items():
        noise = np.random.default_rng([zlib.crc32(name.encode()), seed]).standard_normal(out[name].shape)
        drawn = base * np.exp(spread * noise) if base else spread * noise
        out[name] = jnp.asarray(drawn.astype(out[name].dtype))
    for name, factor in factors.items():
        out[name] = (out[name] * factor).astype(out[name].dtype)
    return out
```

```python
import concourse.bass as bass
from concourse import mybir
from contextlib import ExitStack

N_NODES, F = 3125, 16
N_EDGES, F_EDGE0 = 100000, 8
FF = F * F
LAYERS = 3
P = 128
LO = P // F
HI = 392
NODES = LO * HI
QUARTER = HI // 4
G = 8
TILES = 784
EDGES = TILES * P
GROUPS = TILES // G
ROUNDS = GROUPS // 2
HALF = G // 2
PAD_NODE = NODES - 1
ROWS0, ROWS = 6 * F_EDGE0, 6 * F
KROWS = 112
CH = 1568
CHUNKS0, CHUNKS = EDGES * F_EDGE0 // P // CH, EDGES * F // P // CH
EPS = 1e-5
NORM_MSG = float(1.0 / (F * F_EDGE0) ** 0.5)
NORM_UPD = float(1.0 / (F * F) ** 0.5)
NORM_LIN = float(1.0 / F ** 0.5)
ACT_TILES = (1, 3, 5, 7)
DVE_TILES = tuple(t for t in range(G) if t not in ACT_TILES)


def upto(g, n, k):
    return (g + 2) * n + k


def gnn_kernel(nc, x_rows, x_t, src_i, dst_i, ea0, ea1, w0_rep, w_rep, w_sel0, w_sel, bd_msg, bd_upd,
               bd_root, bias_root, bd_tp, ident_d, iota_d, avg_d, out):
    f32, bf16, i32 = mybir.dt.float32, mybir.dt.bfloat16, mybir.dt.int32
    ALU, ACT, AX = mybir.AluOpType, mybir.ActivationFunctionType, mybir.AxisListType

    table = nc.dram_tensor("node_table", [NODES, F], f32, kind="Internal").ap()
    parts0 = nc.dram_tensor("edge_parts0", [ROWS0, EDGES], bf16, kind="Internal").ap()
    parts1 = nc.dram_tensor("edge_parts1", [ROWS, EDGES], bf16, kind="Internal").ap()

    ctx = ExitStack()
    with ctx:
        def sb(name, shape, dt=f32):
            return ctx.enter_context(nc.sbuf_tensor(name, shape, dt))

        def pb(name, shape, dt=f32):
            return ctx.enter_context(nc.psum_tensor(name, shape, dt))

        def sem(name):
            return ctx.enter_context(nc.semaphore(name))

        ident = sb("ident", [P, P])
        iota = sb("iota", [P, HI])
        avg = sb("avg", [P, P])
        zeros = sb("zeros", [P, HI], bf16)
        eps = sb("eps", [P, 1])
        bdm = sb("bdm", [P, P])
        bdu = sb("bdu", [P, P])
        bdr = sb("bdr", [P, LAYERS, P])
        bdr_now = sb("bdr_now", [P, P])
        br = sb("br", [P, LAYERS])
        br_now = sb("br_now", [P, 1])
        bdt = sb("bdt", [P, LO * FF])
        wraw = sb("wraw", [KROWS, (LAYERS + 1) * FF])
        whi = sb("whi", [KROWS, (LAYERS + 1) * FF], bf16)
        wres = sb("wres", [KROWS, (LAYERS + 1) * FF])
        wmid = sb("wmid", [KROWS, (LAYERS + 1) * FF], bf16)
        wlow = sb("wlow", [KROWS, (LAYERS + 1) * FF], bf16)
        wpart = sb("wpart", [KROWS, (LAYERS + 1) * FF], bf16)
        wsel = sb("wsel", [KROWS, 6])
        w_now = sb("w_now", [KROWS, FF], bf16)
        idx = {k: sb("idx_" + k, [P, TILES], i32) for k in ("src", "dst")}
        tmp_i = sb("tmp_i", [P, TILES], i32)
        lo_f = sb("lo_f", [P, TILES])
        hi_f = {k: sb("hi_" + k, [P, TILES]) for k in ("src", "dst")}
        neg_hi = {k: sb("neg_hi_" + k, [P, TILES]) for k in ("src", "dst")}
        mask = {k: sb("mask_" + k, [P, TILES * LO], bf16) for k in ("src", "dst")}
        row_f = sb("row_f", [P, TILES])
        col_f = sb("col_f", [P, TILES])
        xs = sb("xs", [P, 2, CH])
        xh = sb("xh", [P, 2, CH], bf16)
        xm = sb("xm", [P, 2, CH], bf16)
        xl = sb("xl", [P, 2, CH], bf16)
        pace = sb("pace", [P, 2])
        idx_now = sb("idx_now", [P, 2, G], i32)
        xg = sb("xg", [P, 2, G * F])
        ea = sb("ea", [KROWS, 2, G * P], bf16)
        prod = sb("prod", [P, 2, HALF * FF])
        msg = sb("msg", [P, 2, G * F])
        act_msg = sb("act_msg", [P, 2, G * F])
        spread = sb("spread", [P, 2, G * P])
        onehot = sb("onehot", [P, 2, G, HI])
        dist = sb("dist", [P, len(ACT_TILES), HI])
        crow = sb("crow", [P, G * QUARTER], bf16)
        ccol = sb("ccol", [P, G * 32], bf16)
        x0_t = sb("x0_t", [P, HI])
        x1_t = sb("x1_t", [P, HI])
        h_t = sb("h_t", [P, HI])
        rc_t = sb("rc_t", [P, HI])
        y_t = sb("y_t", [P, HI])
        d_t = sb("d_t", [P, HI])
        sq_t = sb("sq_t", [P, HI])
        std_t = sb("std_t", [P, HI])
        out_t = sb("out_t", [P, HI])
        agg_t = sb("agg_t", [P, HI])
        agl_t = sb("agl_t", [P, HI])
        us_t = sb("us_t", [P, HI])
        agg_n = sb("agg_n", [QUARTER, 4 * P])
        u_n = sb("u_n", [QUARTER, 4 * P])
        us_n = sb("us_n", [QUARTER, 4 * P])
        rc_s = sb("rc_s", [QUARTER, 32])
        rc_n = sb("rc_n", [QUARTER, 4 * P])
        tab_n = sb("tab_n", [QUARTER, 4 * P])

        w_ps = [pb(f"w_ps{h}", [P, HALF * FF]) for h in range(2)]
        acc = pb("acc", [P, 512])
        cnt = pb("cnt", [P, 512])
        q0 = pb("q0", [P, 512])
        q1 = pb("q1", [P, 512])

        names = """loads zeroed prep idx_ready prod_done red_done msg_done silu_done s_ready oh_dve
            oh_act dist_done w_done scat_done cnt_oh cnt_mm wsplit hraw sub1 mid sub2 table_written
            w_copied pass_done agg_ready agl_mm agl_ready aggn_tr aggn_ready tp_mm tp_prod tp_red
            us_ready us_tr ust_ready upd_mm y_ready mean_mm d_ready sq_ready var_mm std_ready
            rstd_ready ln_ready h_ready h_tr tab_ready rc_chain rcn_tr rct_ready root_mm
            scaled out_done"""
        S = {n: sem(n) for n in names.split()}
        chunk_in = [sem(f"chunk_in{b}") for b in range(2)]
        chunk_out = [sem(f"chunk_out{b}") for b in range(2)]
        gathered = [sem(f"gathered{b}") for b in range(2)]
        ea_in = [sem(f"ea_in{b}") for b in range(2)]

        block = ctx.enter_context(nc.Block())
        N_LOADS = 19

        @block.sync
        def _(sp):
            for dst, src in (
                (idx["src"][:], src_i), (idx["dst"][:], dst_i), (ident[:], ident_d), (iota[:], iota_d),
                (avg[:], avg_d), (bdm[:], bd_msg), (bdu[:], bd_upd), (bdt[:], bd_tp),
                (bdr[:, 0, :], bd_root[0]), (bdr[:, 1, :], bd_root[1]), (bdr[:, 2, :], bd_root[2]),
                (br[:], bias_root), (x0_t[:], x_t), (wsel[:, 0:3], w_sel0), (wsel[:, 3:6], w_sel),
                (wraw[:, 0:FF], w0_rep), (wraw[:, FF:2 * FF], w_rep[0]),
                (wraw[:, 2 * FF:3 * FF], w_rep[1]), (wraw[:, 3 * FF:4 * FF], w_rep[2]),
            ):
                sp.dma_start(dst, src).then_inc(S["loads"], 16)
            flat = [(ea0, parts0, c, 8 * CHUNKS0) for c in range(CHUNKS0)] + [(ea1, parts1, c, 0) for c in range(CHUNKS)]

            def store(c):
                b = c % 2
                whole, to, k, _ = flat[c]
                rows = to.shape[0] // 6
                sp.wait_ge(S["sub2"], c + 1)
                for block_, part in enumerate((xh, xh, xh, xm, xm, xl)):
                    view = to[block_ * rows:(block_ + 1) * rows, :].rearrange("i (q c) -> (i q) c", q=P // rows)
                    sp.dma_start(view[:, k * CH:(k + 1) * CH], part[:, b, :]).then_inc(chunk_out[b], 16)

            for c, (whole, to, k, _) in enumerate(flat):
                b = c % 2
                if c >= 2:
                    sp.wait_ge(S["sub2"], c - 1)
                sp.dma_start(xs[:, b, :], whole[:, k * CH:(k + 1) * CH]).then_inc(chunk_in[b], 16)
                if c >= 1:
                    store(c - 1)
            store(len(flat) - 1)
            for b in range(2):
                sp.wait_ge(chunk_out[b], 96 * (len(flat) // 2))
            sp.wait_ge(S["zeroed"], 1)

            def load_group(parts, rows, g, local, b):
                sp.wait_ge(S["w_done"], upto(g, 2, 0) - 2)
                sp.dma_start(ea[0:rows, b, :], parts[:, bass.ds(local * (G * P), G * P)]).then_inc(ea_in[b], 16)

            with sp.Fori(0, ROUNDS) as i:
                for b in range(2):
                    load_group(parts0, ROWS0, i * 2 + b, i * 2 + b, b)
            with sp.Fori(0, LAYERS) as l:
                with sp.Fori(0, ROUNDS) as i:
                    for b in range(2):
                        load_group(parts1, ROWS, l * GROUPS + i * 2 + (GROUPS + b), i * 2 + b, b)
                sp.wait_ge(S["tab_ready"], l + 2)
                sp.dma_start(table.rearrange("(p n) f -> p (n f)", n=32), tab_n[:]).then_inc(S["table_written"], 16)
            sp.wait_ge(S["ln_ready"], 2)
            sp.dma_start(out, out_t[:]).then_inc(S["out_done"], 16)
            sp.wait_ge(S["table_written"], 16 * (LAYERS + 1))
            sp.wait_ge(S["out_done"], 16)

        @block.gpsimd
        def _(pool):
            pool.wait_ge(S["loads"], 16 * N_LOADS)
            nc.gpsimd.memset(pace[:], 0.0).then_inc(S["idx_ready"], 1)

            def gather_group(rows, which, g, u, local, b):
                pool.wait_ge(gathered[b], u * (16 * G))
                pool.wait_ge(S["prod_done"], upto(g, 2, 0) - 2)
                pool.wait_ge(S["idx_ready"], g * 2 + 1)
                nc.gpsimd.tensor_copy(idx_now[:, b, :], idx[which][:, bass.ds(local * G, G)]).then_inc(S["idx_ready"], 1)
                pool.wait_ge(S["idx_ready"], g * 2 + 2)
                nc.gpsimd.tensor_tensor(pace[:, 1:2], pace[:, 0:1], pace[:, 0:1], ALU.add).then_inc(S["idx_ready"], 1)
                for t in range(G):
                    pool.indirect_dma_start(
                        out=xg[:, b, t * F:(t + 1) * F], out_offset=None, in_=rows,
                        in_offset=bass.IndirectOffsetOnAxis(ap=idx_now[:, b, t:t + 1], axis=0),
                    ).then_inc(gathered[b], 16)

            with pool.Fori(0, ROUNDS) as i:
                for b in range(2):
                    gather_group(x_rows, "dst", i * 2 + b, i, i * 2 + b, b)
            with pool.Fori(0, LAYERS) as l:
                with pool.Fori(0, ROUNDS) as i:
                    pool.wait_ge(S["table_written"], l * 16 + 16)
                    for b in range(2):
                        gather_group(table, "src", l * GROUPS + i * 2 + (GROUPS + b),
                                     l * ROUNDS + i + ROUNDS, i * 2 + b, b)

        @block.vector
        def _(dve):
            for n, k in (("prod_done", 4), ("red_done", 4), ("s_ready", 2), ("oh_dve", 2), ("cnt_oh", 2)):
                dve.sem_inc(S[n], k)
            nc.vector.memset(ea[:], 0.0).then_inc(S["prep"], 1)
            nc.vector.memset(zeros[:], 0.0)
            nc.vector.memset(eps[:], EPS)
            dve.wait_ge(S["prep"], 1)
            nc.vector.memset(ea[96:KROWS, :, :], 1.0).then_inc(S["zeroed"], 1)
            dve.wait_ge(S["loads"], 16 * N_LOADS)
            made = [1]

            def link(ins):
                made[0] += 1
                ins.then_inc(S["prep"], 1)
                dve.wait_ge(S["prep"], made[0])

            iota_lo = iota[:, 0:LO].unsqueeze(1).broadcast_to([P, TILES, LO])
            for k in ("src", "dst"):
                link(nc.vector.tensor_scalar(tmp_i[:], idx[k][:], LO - 1, None, ALU.bitwise_and))
                link(nc.vector.tensor_copy(lo_f[:], tmp_i[:]))
                link(nc.vector.tensor_tensor(mask[k][:].rearrange("p (t a) -> p t a", a=LO),
                                             lo_f[:].unsqueeze(2).broadcast_to([P, TILES, LO]), iota_lo, ALU.is_equal))
                link(nc.vector.tensor_scalar(tmp_i[:], idx[k][:], 3, None, ALU.arith_shift_right))
                link(nc.vector.tensor_copy(hi_f[k][:], tmp_i[:]))
                link(nc.vector.tensor_scalar(neg_hi[k][:], hi_f[k][:], -1.0, None, ALU.mult))
            link(nc.vector.tensor_scalar(tmp_i[:], idx["dst"][:], 5, None, ALU.arith_shift_right))
            link(nc.vector.tensor_copy(row_f[:], tmp_i[:]))
            link(nc.vector.tensor_scalar(tmp_i[:], idx["dst"][:], 31, None, ALU.bitwise_and))
            link(nc.vector.tensor_copy(col_f[:], tmp_i[:]))
            link(nc.vector.tensor_copy(whi[:], wraw[:]))
            link(nc.vector.tensor_tensor(wres[:], wraw[:], whi[:], ALU.subtract))
            link(nc.vector.tensor_copy(wmid[:], wres[:]))
            link(nc.vector.tensor_tensor(wlow[:], wres[:], wmid[:], ALU.subtract))
            for a, b_, k in ((0, FF, 0), (FF, (LAYERS + 1) * FF, 3)):
                link(nc.vector.tensor_scalar(wpart[:, a:b_], whi[:, a:b_], wsel[:, k:k + 1], None, ALU.mult))
                for part, j in ((wmid, 1), (wlow, 2)):
                    link(nc.vector.scalar_tensor_tensor(out=wpart[:, a:b_], in0=part[:, a:b_], scalar=wsel[:, k + j:k + j + 1],
                                                        in1=wpart[:, a:b_], op0=ALU.mult, op1=ALU.add))
            nc.vector.tensor_copy(w_now[:], wpart[:, 0:FF]).then_inc(S["wsplit"], 1)

            for c in range(CHUNKS0 + CHUNKS):
                b = c % 2
                dve.wait_ge(S["hraw"], c + 1)
                nc.vector.tensor_tensor(xs[:, b, :], xs[:, b, :], xh[:, b, :], ALU.subtract).then_inc(S["sub1"], 1)
                dve.wait_ge(S["mid"], c + 1)
                if c >= 2:
                    dve.wait_ge(chunk_out[b], 96 * (c // 2))
                nc.vector.tensor_tensor(xl[:, b, :], xs[:, b, :], xm[:, b, :], ALU.subtract).then_inc(S["sub2"], 1)

            def products(g, u, b, h, relu):
                dve.wait_ge(gathered[b], u * (16 * G) + 16 * G)
                dve.wait_ge(S["w_done"], upto(g, 2, h + 1))
                dve.wait_ge(S["red_done"], upto(g, 2, h + 1) - 2)
                w = w_ps[h][:].rearrange("p (i o) -> p i o", o=F)
                xin = xg[:, b, h * HALF * F:(h + 1) * HALF * F].unsqueeze(2).broadcast_to([P, HALF * F, F])
                o = prod[:, h, :].rearrange("p (i o) -> p i o", o=F)
                if relu:
                    ins = nc.vector.scalar_tensor_tensor(out=o, in0=w, scalar=0.0, in1=xin, op0=ALU.max, op1=ALU.mult)
                else:
                    ins = nc.vector.tensor_tensor(o, w, xin, ALU.mult)
                ins.then_inc(S["prod_done"], 1)

            def reduce_half(g, b, h, free):
                dve.wait_ge(S["prod_done"], upto(g, 2, h + 1))
                dve.wait_ge(free, upto(g, 1, 0) - 1)
                nc.vector.tensor_reduce(
                    out=msg[:, b, h * HALF * F:(h + 1) * HALF * F].rearrange("p (t o) -> p t o", o=F),
                    in_=prod[:, h, :].rearrange("p (t i o) -> p t o i", i=F, o=F), axis=AX.X, op=ALU.add,
                ).then_inc(S["red_done"], 1)

            def one_hot(g, local, b, which, t, last):
                ins = nc.vector.tensor_scalar(onehot[:, b, t, :], iota[:], hi_f[which][:, bass.ds(local * G + t, 1)],
                                              None, ALU.is_equal)
                if last:
                    ins.then_inc(S["oh_dve"], 1)

            def spread_group(g, local, b, which, source):
                nc.vector.tensor_tensor(
                    spread[:, b, :].rearrange("p (t a o) -> p t a o", a=LO, o=F),
                    mask[which][:, bass.ds(local * (G * LO), G * LO)].rearrange("p (t a) -> p t a", a=LO)
                    .unsqueeze(3).broadcast_to([P, G, LO, F]),
                    source[:, b, :].rearrange("p (t o) -> p t o", o=F).unsqueeze(2).broadcast_to([P, G, LO, F]),
                    ALU.mult).then_inc(S["s_ready"], 1)

            def group(g, u, local, b, which, first_pass):
                free = S["silu_done"] if first_pass else S["s_ready"]
                n = len(DVE_TILES)
                products(g, u, b, 0, not first_pass)
                dve.wait_ge(S["scat_done"], upto(g, 1, 0) - 1)
                one_hot(g, local, b, which, DVE_TILES[0], False)
                products(g, u, b, 1, not first_pass)
                for t in DVE_TILES[1:n - 2]:
                    one_hot(g, local, b, which, t, False)
                reduce_half(g, b, 0, free)
                one_hot(g, local, b, which, DVE_TILES[n - 2], False)
                reduce_half(g, b, 1, free)
                one_hot(g, local, b, which, DVE_TILES[n - 1], True)
                if first_pass:
                    dve.wait_ge(S["cnt_mm"], g + 1)
                    for o, f, w in ((crow, row_f, QUARTER), (ccol, col_f, 32)):
                        ins = nc.vector.tensor_tensor(
                            o[:].rearrange("p (t w) -> p t w", w=w),
                            f[:, bass.ds(local * G, G)].unsqueeze(2).broadcast_to([P, G, w]),
                            iota[:, 0:w].unsqueeze(1).broadcast_to([P, G, w]), ALU.is_equal)
                    ins.then_inc(S["cnt_oh"], 1)
                    dve.wait_ge(S["silu_done"], upto(g, 1, 1))
                else:
                    dve.wait_ge(S["red_done"], upto(g, 2, 2))
                spread_group(g, local, b, which, act_msg if first_pass else msg)

            with dve.Fori(0, ROUNDS) as i:
                for b in range(2):
                    group(i * 2 + b, i, i * 2 + b, b, "src", True)

            dve.wait_ge(S["pass_done"], 1)
            nc.vector.tensor_scalar(rc_s[:], cnt[0:QUARTER, 0:32], 1.0, None, ALU.max).then_inc(S["rc_chain"], 1)
            dve.wait_ge(S["rc_chain"], 1)
            nc.vector.reciprocal(rc_s[:], rc_s[:]).then_inc(S["rc_chain"], 1)
            dve.wait_ge(S["rc_chain"], 2)
            nc.vector.tensor_copy(rc_n[:].rearrange("p (m f) -> p m f", f=F),
                                  rc_s[:].unsqueeze(2).broadcast_to([QUARTER, 32, F])).then_inc(S["rc_chain"], 1)

            dve.wait_ge(S["aggn_ready"], 1)
            for k in range(8):
                h = k % 2
                dve.wait_ge(S["tp_mm"], k + 1)
                if k >= 2:
                    dve.wait_ge(S["tp_red"], k - 1)
                nc.vector.tensor_tensor(
                    prod[0:QUARTER, h, :].rearrange("p (i o) -> p i o", o=F),
                    w_ps[h][0:QUARTER, :].rearrange("p (i o) -> p i o", o=F),
                    agg_n[:, k * HALF * F:(k + 1) * HALF * F].unsqueeze(2).broadcast_to([QUARTER, HALF * F, F]),
                    ALU.mult).then_inc(S["tp_prod"], 1)
                dve.wait_ge(S["tp_prod"], k + 1)
                nc.vector.tensor_reduce(
                    out=u_n[:, k * HALF * F:(k + 1) * HALF * F].rearrange("p (t o) -> p t o", o=F),
                    in_=prod[0:QUARTER, h, :].rearrange("p (t i o) -> p t o i", i=F, o=F), axis=AX.X,
                    op=ALU.add).then_inc(S["tp_red"], 1)
            dve.wait_ge(S["upd_mm"], 1)
            nc.vector.scalar_tensor_tensor(out=y_t[:], in0=q0[:, 0:HI], scalar=NORM_LIN, in1=x0_t[:],
                                           op0=ALU.mult, op1=ALU.add).then_inc(S["scaled"], 1)
            dve.wait_ge(S["scaled"], 1)
            nc.vector.tensor_tensor(y_t[:], y_t[:], x0_t[:], ALU.add).then_inc(S["y_ready"], 1)

            def layer_norm(n, to):
                dve.wait_ge(S["mean_mm"], n)
                nc.vector.tensor_tensor(d_t[:], y_t[:], q0[:, 0:HI], ALU.subtract).then_inc(S["d_ready"], 1)
                dve.wait_ge(S["std_ready"], n)
                nc.vector.reciprocal(std_t[:], std_t[:]).then_inc(S["rstd_ready"], 1)
                dve.wait_ge(S["rstd_ready"], n)
                nc.vector.tensor_tensor(to[:], d_t[:], std_t[:], ALU.mult).then_inc(S["ln_ready"], 1)

            layer_norm(1, x1_t)
            dve.wait_ge(S["ln_ready"], 1)
            nc.vector.tensor_copy(h_t[:], x1_t[:]).then_inc(S["h_ready"], 1)

            with dve.Fori(0, LAYERS) as l:
                with dve.Fori(0, ROUNDS) as i:
                    for b in range(2):
                        group(l * GROUPS + i * 2 + (GROUPS + b), l * ROUNDS + i + ROUNDS, i * 2 + b, b, "dst", False)
                dve.wait_ge(S["rct_ready"], 1)
                dve.wait_ge(S["root_mm"], l + 1)
                nc.vector.tensor_tensor(y_t[:], acc[:, 0:HI], rc_t[:], ALU.mult).then_inc(S["scaled"], 1)
                dve.wait_ge(S["scaled"], l + 2)
                nc.vector.scalar_tensor_tensor(out=h_t[:], in0=q0[:, 0:HI], scalar=br_now[:], in1=y_t[:],
                                               op0=ALU.add, op1=ALU.add).then_inc(S["h_ready"], 1)
            dve.wait_ge(S["h_ready"], LAYERS + 1)
            nc.vector.tensor_tensor(y_t[:], h_t[:], x1_t[:], ALU.add).then_inc(S["y_ready"], 1)
            layer_norm(2, out_t)

        @block.scalar
        def _(act):
            for n, k in (("oh_act", 2), ("silu_done", 2)):
                act.sem_inc(S[n], k)
            act.wait_ge(S["loads"], 16 * N_LOADS)
            for c in range(CHUNKS0 + CHUNKS):
                b = c % 2
                act.wait_ge(chunk_in[b], 16 * (c // 2 + 1))
                if c >= 2:
                    act.wait_ge(chunk_out[b], 96 * (c // 2))
                nc.scalar.activation(xh[:, b, :], xs[:, b, :], ACT.Copy).then_inc(S["hraw"], 1)
                act.wait_ge(S["sub1"], c + 1)
                nc.scalar.activation(xm[:, b, :], xs[:, b, :], ACT.Copy).then_inc(S["mid"], 1)

            def one_hots(g, local, b, which):
                act.wait_ge(S["oh_act"], upto(g, 1, 0))
                act.wait_ge(S["loads"], 16 * N_LOADS)
                for j, t in enumerate(ACT_TILES):
                    nc.scalar.activation(dist[:, j, :], iota[:], ACT.Abs,
                                         bias=neg_hi[which][:, bass.ds(local * G + t, 1)]).then_inc(S["dist_done"], 1)
                act.wait_ge(S["scat_done"], upto(g, 1, 0) - 1)
                for j, t in enumerate(ACT_TILES):
                    act.wait_ge(S["dist_done"], g * len(ACT_TILES) + (j + 1))
                    ins = nc.scalar.activation(onehot[:, b, t, :], dist[:, j, :], ACT.Relu, scale=-1.0, bias=1.0)
                ins.then_inc(S["oh_act"], 1)

            def silu_group(g, b):
                act.wait_ge(S["red_done"], upto(g, 2, 2))
                act.wait_ge(S["s_ready"], upto(g, 1, 0) - 1)
                nc.scalar.activation(act_msg[:, b, :], msg[:, b, :], ACT.Silu, scale=NORM_MSG).then_inc(S["silu_done"], 1)

            with act.Fori(0, ROUNDS) as i:
                for b in range(2):
                    one_hots(i * 2 + b, i * 2 + b, b, "src")
                    silu_group(i * 2 + b, b)

            act.wait_ge(S["pass_done"], 1)
            nc.scalar.activation(agg_t[:], acc[:, 0:HI], ACT.Copy).then_inc(S["agg_ready"], 1)
            act.wait_ge(S["agl_mm"], 1)
            nc.scalar.activation(agl_t[:], q0[:, 0:HI], ACT.Copy, scale=NORM_LIN).then_inc(S["agl_ready"], 1)
            act.wait_ge(S["aggn_tr"], 1)
            nc.scalar.activation(agg_n[:], q1[0:QUARTER, :], ACT.Copy).then_inc(S["aggn_ready"], 1)
            act.wait_ge(S["rcn_tr"], 1)
            nc.scalar.activation(rc_t[:].rearrange("q (p c) -> q c p", c=4),
                                 q0[:, 0:HI].rearrange("q (c p) -> q c p", c=4), ACT.Copy).then_inc(S["rct_ready"], 1)
            act.wait_ge(S["tp_red"], 8)
            nc.scalar.activation(us_n[:], u_n[:], ACT.Silu, scale=NORM_UPD).then_inc(S["us_ready"], 1)
            act.wait_ge(S["us_tr"], 1)
            nc.scalar.activation(us_t[:].rearrange("q (p c) -> q c p", c=4),
                                 q1[:, 0:HI].rearrange("q (c p) -> q c p", c=4), ACT.Copy).then_inc(S["ust_ready"], 1)

            def layer_norm(n):
                act.wait_ge(S["d_ready"], n)
                nc.scalar.activation(sq_t[:], d_t[:], ACT.Square).then_inc(S["sq_ready"], 1)
                act.wait_ge(S["var_mm"], n)
                nc.scalar.activation(std_t[:], q1[:, 0:HI], ACT.Sqrt, bias=eps[:]).then_inc(S["std_ready"], 1)

            layer_norm(1)
            act.wait_ge(S["h_tr"], 1)
            nc.scalar.activation(tab_n[:], q1[0:QUARTER, :], ACT.Copy).then_inc(S["tab_ready"], 1)
            act.wait_ge(S["tab_ready"], 1)
            act.dma_start(table.rearrange("(p n) f -> p (n f)", n=32), tab_n[:]).then_inc(S["table_written"], 16)

            with act.Fori(0, LAYERS) as l:
                act.wait_ge(S["h_ready"], l + 1)
                act.wait_ge(S["loads"], 16 * N_LOADS)
                nc.scalar.activation(w_now[:], wpart[:, bass.ds(l * FF + FF, FF)], ACT.Copy)
                nc.scalar.activation(bdr_now[:], bdr[:].rearrange("p l c -> p (l c)")[:, bass.ds(l * P, P)], ACT.Copy)
                nc.scalar.activation(br_now[:], br[:, bass.ds(l, 1)], ACT.Copy).then_inc(S["w_copied"], 1)
                with act.Fori(0, ROUNDS) as i:
                    for b in range(2):
                        one_hots(l * GROUPS + i * 2 + (GROUPS + b), i * 2 + b, b, "dst")
                act.wait_ge(S["h_tr"], l + 2)
                act.wait_ge(S["table_written"], l * 16 + 16)
                nc.scalar.activation(tab_n[:], q1[0:QUARTER, :], ACT.Copy).then_inc(S["tab_ready"], 1)
            layer_norm(2)

        @block.tensor
        def _(pe):
            for n, k in (("w_done", 4), ("scat_done", 2), ("cnt_mm", 1)):
                pe.sem_inc(S[n], k)
            pe.wait_ge(S["loads"], 16 * N_LOADS)
            pe.wait_ge(S["wsplit"], 1)

            def weights(g, u, b):
                pe.wait_ge(ea_in[b], u * 16 + 16)
                for h in range(2):
                    pe.wait_ge(S["prod_done"], upto(g, 2, h + 1) - 2)
                    for j in range(HALF):
                        t = h * HALF + j
                        last = nc.tensor.matmul(w_ps[h][:, j * FF:(j + 1) * FF], ea[:, b, t * P:(t + 1) * P],
                                                w_now[:], start=True, stop=True)
                    last.then_inc(S["w_done"], 1)

            def scatter(g, b, counts):
                if counts:
                    pe.wait_ge(S["cnt_oh"], upto(g, 1, 1))
                    for t in range(G):
                        last = nc.tensor.matmul(cnt[0:QUARTER, 0:32], crow[:, t * QUARTER:(t + 1) * QUARTER],
                                                ccol[:, t * 32:(t + 1) * 32], start=False, stop=False)
                    last.then_inc(S["cnt_mm"], 1)
                pe.wait_ge(S["s_ready"], upto(g, 1, 1))
                pe.wait_ge(S["oh_dve"], upto(g, 1, 1))
                pe.wait_ge(S["oh_act"], upto(g, 1, 1))
                for t in range(G):
                    last = nc.tensor.matmul(acc[:, 0:HI], spread[:, b, t * P:(t + 1) * P], onehot[:, b, t, :],
                                            start=False, stop=False)
                last.then_inc(S["scat_done"], 1)

            def edge_pass(g0, u0, counts):
                nc.tensor.matmul(acc[:, 0:HI], zeros[:, 0:P], zeros[:, 0:HI], start=True, stop=False)
                if counts:
                    nc.tensor.matmul(cnt[0:QUARTER, 0:32], zeros[:, 0:QUARTER], zeros[:, 0:32], start=True, stop=False)
                weights(g0, u0, 0)
                with pe.Fori(0, ROUNDS - 1) as i:
                    weights(i * 2 + g0 + 1, i + u0, 1)
                    scatter(i * 2 + g0, 0, counts)
                    weights(i * 2 + g0 + 2, i + u0 + 1, 0)
                    scatter(i * 2 + g0 + 1, 1, counts)
                weights(g0 + (GROUPS - 1), u0 + (ROUNDS - 1), 1)
                scatter(g0 + (GROUPS - 2), 0, counts)
                scatter(g0 + (GROUPS - 1), 1, counts)
                if counts:
                    nc.tensor.matmul(cnt[0:QUARTER, 0:32], zeros[:, 0:QUARTER], zeros[:, 0:32], start=False, stop=True)
                nc.tensor.matmul(acc[:, 0:HI], zeros[:, 0:P], zeros[:, 0:HI], start=False,
                                 stop=True).then_inc(S["pass_done"], 1)

            def to_rows(of, done):
                view = of[:].rearrange("q (p c) -> q c p", c=4)
                for c in range(4):
                    last = nc.tensor.transpose(q1[0:QUARTER, c * P:(c + 1) * P], view[:, c, :], ident[:])
                last.then_inc(done, 1)

            def to_columns(to, of, done):
                for c in range(4):
                    last = nc.tensor.transpose(to[:, c * QUARTER:(c + 1) * QUARTER], of[:, c * P:(c + 1) * P],
                                               ident[0:QUARTER, 0:QUARTER])
                last.then_inc(done, 1)

            def layer_norm(n):
                pe.wait_ge(S["y_ready"], n)
                nc.tensor.matmul(q0[:, 0:HI], avg[:], y_t[:], start=True, stop=True).then_inc(S["mean_mm"], 1)
                pe.wait_ge(S["sq_ready"], n)
                nc.tensor.matmul(q1[:, 0:HI], avg[:], sq_t[:], start=True, stop=True).then_inc(S["var_mm"], 1)

            edge_pass(0, 0, True)
            pe.wait_ge(S["agg_ready"], 1)
            nc.tensor.matmul(q0[:, 0:HI], bdm[:], agg_t[:], start=True, stop=True).then_inc(S["agl_mm"], 1)
            pe.wait_ge(S["agl_ready"], 1)
            to_rows(agl_t, S["aggn_tr"])
            x_view = x0_t[:].rearrange("q (p c) -> q c p", c=4)
            for k in range(8):
                c, h = k // 2, k % 2
                if k >= 2:
                    pe.wait_ge(S["tp_prod"], k - 1)
                for j in range(2):
                    at = h * HALF * FF + j * 512
                    last = nc.tensor.matmul(w_ps[h][0:QUARTER, j * 512:(j + 1) * 512], x_view[:, c, :],
                                            bdt[:, at:at + 512], start=True, stop=True)
                last.then_inc(S["tp_mm"], 1)
            pe.wait_ge(S["rc_chain"], 3)
            to_columns(q0, rc_n, S["rcn_tr"])
            pe.wait_ge(S["us_ready"], 1)
            to_columns(q1, us_n, S["us_tr"])
            pe.wait_ge(S["ust_ready"], 1)
            pe.wait_ge(S["rct_ready"], 1)
            nc.tensor.matmul(q0[:, 0:HI], bdu[:], us_t[:], start=True, stop=True).then_inc(S["upd_mm"], 1)
            layer_norm(1)
            pe.wait_ge(S["h_ready"], 1)
            to_rows(h_t, S["h_tr"])

            with pe.Fori(0, LAYERS) as l:
                pe.wait_ge(S["w_copied"], l + 1)
                edge_pass(l * GROUPS + GROUPS, l * ROUNDS + ROUNDS, False)
                nc.tensor.matmul(q0[:, 0:HI], bdr_now[:], h_t[:], start=True, stop=True).then_inc(S["root_mm"], 1)
                pe.wait_ge(S["h_ready"], l + 2)
                to_rows(h_t, S["h_tr"])
            pe.wait_ge(S["tab_ready"], LAYERS + 1)
            layer_norm(2)


def kernel(**inputs):
    import numpy as np
    import concourse.bacc as bacc
    from concourse.bass_utils import run_bass_kernel_spmd as run

    a = {k: np.asarray(v) for k, v in inputs.items()}
    f4 = np.float32

    def blocks(w):
        o = np.zeros((P, LO * w.shape[1]), w.dtype)
        for k in range(LO):
            o[k * F:(k + 1) * F, k * w.shape[1]:(k + 1) * w.shape[1]] = w
        return o

    def rows(w, bias=None):
        o = np.zeros((KROWS, FF), w.dtype)
        for k in range(6):
            o[k * w.shape[0]:(k + 1) * w.shape[0]] = w
        if bias is not None:
            o[96:99] = bias
        return o

    def select(r, bias):
        o = np.zeros((KROWS, 3), f4)
        for k, part in enumerate((0, 1, 2, 0, 1, 0)):
            o[k * r:(k + 1) * r, part] = 1.0
        if bias:
            o[96:99] = np.eye(3, dtype=f4)
        return o

    def indices(v):
        o = np.full(EDGES, PAD_NODE, np.int32)
        o[:N_EDGES] = v
        return np.ascontiguousarray(o.reshape(TILES, P).T)

    def flat(v):
        o = np.zeros((v.shape[1], EDGES), v.dtype)
        o[:, :N_EDGES] = v.T
        return o.reshape(P, -1)

    x = np.zeros((NODES, F), a["x"].dtype)
    x[:N_NODES] = a["x"]
    tp0 = a["L0_gnn_W_msg_tp"].transpose(1, 0, 2).reshape(F_EDGE0, FF)
    upd = a["L0_gnn_W_upd_tp"].reshape(F, FF)
    layers = ("1", "2", "3")
    arrays = {
        "x_rows": x,
        "x_t": np.ascontiguousarray(x.reshape(HI, LO * F).T),
        "src": indices(a["src"]), "dst": indices(a["dst"]),
        "ea0": flat(a["edge_attr_8"]), "ea1": flat(a["edge_attr_16"]),
        "w0": rows(tp0),
        "w": np.stack([rows(a[f"L1_gnn_Wn{k}"], a[f"L1_gnn_bn{k}"]) for k in layers]),
        "sel0": select(F_EDGE0, False), "sel": select(F, True),
        "bd_msg": blocks(a["L0_gnn_W_msg_lin"]), "bd_upd": blocks(a["L0_gnn_W_upd_lin"]),
        "bd_root": np.stack([blocks(a[f"L1_gnn_Wr{k}"]) for k in layers]),
        "bias_root": np.ascontiguousarray(np.stack([np.tile(a[f"L1_gnn_b{k}"], LO) for k in layers]).T),
        "bd_tp": blocks(upd),
        "ident": np.eye(P, dtype=f4),
        "iota": np.tile(np.arange(HI, dtype=f4), (P, 1)),
        "avg": np.kron(np.eye(LO, dtype=f4), np.full((F, F), 1.0 / F, f4)),
    }
    arrays = {f"in_{k}": np.ascontiguousarray(v) for k, v in arrays.items()}
    nc = bacc.Bacc("TRN2", target_bir_lowering=False, num_devices=1)
    args = [nc.dram_tensor(k, v.shape, mybir.dt.from_np(v.dtype), kind="ExternalInput").ap() for k, v in arrays.items()]
    out = nc.dram_tensor("out_nodes", (P, HI), mybir.dt.float32, kind="ExternalOutput").ap()
    gnn_kernel(nc, *args, out)
    got = run(nc, [arrays], core_ids=[0]).results[0]["out_nodes"]
    return np.ascontiguousarray(got.T.reshape(NODES, F)[:N_NODES])
```

```python
import concourse.bass as bass
from concourse import mybir
from contextlib import ExitStack

N_NODES, F = 3125, 16
N_EDGES, F_EDGE0 = 100000, 8
FF = F * F
LAYERS = 3
P = 128
LO = P // F
HI = 392
NODES = LO * HI
QUARTER = HI // 4
G = 8
TILES = 784
EDGES = TILES * P
GROUPS = TILES // G
ROUNDS = GROUPS // 2
HALF = G // 2
PAD_NODE = NODES - 1
ROWS0, ROWS = 6 * F_EDGE0, 6 * F
KROWS = 112
CH0 = 1568
CHUNKS0 = EDGES * F_EDGE0 // P // CH0
CH1 = EDGES * F // P // ROUNDS
EPS = 1e-5
NORM_MSG = float(1.0 / (F * F_EDGE0) ** 0.5)
NORM_UPD = float(1.0 / (F * F) ** 0.5)
NORM_LIN = float(1.0 / F ** 0.5)
PREP_STEPS = 1 + 2 + 7 + 12 + 4
ACT_TILES = ((1, 3, 4, 5, 6, 7), (1, 3, 4, 5, 6, 7))
FETCHED = G - 1


def upto(g, n, k):
    return (g + 2) * n + k


def gathers_done(u, h, layers):
    if h == 0 or not layers:
        return u * (16 * HALF) + 16 * HALF
    return u * (16 * (HALF - 1)) + 16 * (HALF - 1) + 16 * ROUNDS


def gnn_kernel(nc, x_rows, x_t, src_i, dst_i, ea0, ea1, w0_rep, w_rep, w_sel0, w_sel, bd_msg, bd_upd,
               bd_root, bias_root, bd_tp, ident_d, iota_d, avg_d, src_last, column_d, out):
    f32, bf16, f16, i32 = mybir.dt.float32, mybir.dt.bfloat16, mybir.dt.float16, mybir.dt.int32
    ALU, ACT, AX = mybir.AluOpType, mybir.ActivationFunctionType, mybir.AxisListType

    table = nc.dram_tensor("node_table", [NODES, F], f32, kind="Internal").ap()
    parts0 = nc.dram_tensor("edge_parts0", [ROWS0, EDGES], bf16, kind="Internal").ap()
    parts1 = nc.dram_tensor("edge_parts1", [ROWS, EDGES], bf16, kind="Internal").ap()
    hi_rows = nc.dram_tensor("hi_rows", [GROUPS + 2, P], f16, kind="Internal").ap()
    columns = nc.dram_tensor("one_hot_columns", [QUARTER, GROUPS * 4 * P], bf16, kind="Internal").ap()

    ctx = ExitStack()
    with ctx:
        def sb(name, shape, dt=f32):
            return ctx.enter_context(nc.sbuf_tensor(name, shape, dt))

        def pb(name, shape, dt=f32):
            return ctx.enter_context(nc.psum_tensor(name, shape, dt))

        def sem(name):
            return ctx.enter_context(nc.semaphore(name))

        ident = sb("ident", [P, P])
        iota = sb("iota", [P, HI])
        avg = sb("avg", [P, P])
        zeros = sb("zeros", [P, HI], bf16)
        eps = sb("eps", [P, 1])
        bdm = sb("bdm", [P, P])
        bdu = sb("bdu", [P, P])
        bdr = sb("bdr", [P, LAYERS, P])
        bdr_now = sb("bdr_now", [P, P])
        br = sb("br", [P, LAYERS])
        br_now = sb("br_now", [P, 1])
        bdt = sb("bdt", [P, LO * FF])
        wraw = sb("wraw", [KROWS, (LAYERS + 1) * FF])
        whi = sb("whi", [KROWS, (LAYERS + 1) * FF], bf16)
        wres = sb("wres", [KROWS, (LAYERS + 1) * FF])
        wmid = sb("wmid", [KROWS, (LAYERS + 1) * FF], bf16)
        wlow = sb("wlow", [KROWS, (LAYERS + 1) * FF], bf16)
        wpart = sb("wpart", [KROWS, (LAYERS + 1) * FF], bf16)
        wsel = sb("wsel", [KROWS, 6])
        w_now = sb("w_now", [KROWS, FF], bf16)
        idx = {k: sb("idx_" + k, [P, TILES + 2 * G], i32) for k in ("src", "dst")}
        tmp_i = sb("tmp_i", [P, TILES], i32)
        lo_f = sb("lo_f", [P, TILES])
        hi_f = {k: sb("hi_" + k, [P, TILES]) for k in ("src", "dst")}
        neg_hi = {k: sb("neg_hi_" + k, [P, TILES]) for k in ("src", "dst")}
        mask = {k: sb("mask_" + k, [P, TILES * LO], bf16) for k in ("src", "dst")}
        row_f = sb("row_f", [P, TILES])
        col_f = sb("col_f", [P, TILES])
        xs = sb("xs", [P, 2, CH0])
        xh = sb("xh", [P, 2, CH0], bf16)
        xm = sb("xm", [P, 2, CH0], bf16)
        xl = sb("xl", [P, 2, CH0], bf16)
        ys = sb("ys", [P, CH1])
        yh = sb("yh", [P, CH1], bf16)
        ym = sb("ym", [P, CH1], bf16)
        yl = sb("yl", [P, CH1], bf16)
        idx_now = sb("idx_now", [P, 2, G], i32)
        last_i = sb("last_i", [GROUPS + 2, P], i32)
        last_hi = sb("last_hi", [GROUPS + 2, P], f16)
        hi_all = sb("hi_all", [QUARTER, 2 * P], f16)
        column_of = sb("column_of", [QUARTER, 4])
        cols_new = sb("cols_new", [QUARTER, 2, 4, P], bf16)
        cols_now = sb("cols_now", [QUARTER, 2, 4 * P], bf16)
        tab_parts = sb("tab_parts", [QUARTER, 3, 4 * P], bf16)
        picks = sb("picks", [P, P])
        xg = sb("xg", [P, 2, G * F])
        ea = sb("ea", [KROWS, 2, G * P], bf16)
        prod = sb("prod", [P, 2, HALF * FF])
        msg = sb("msg", [P, 2, G * F])
        act_msg = sb("act_msg", [P, 2, G * F])
        spread = sb("spread", [P, 2, G * P])
        onehot = sb("onehot", [P, 2, G, HI])
        dist = xs[:].rearrange("p b c -> p (b c)")[:, 0:len(ACT_TILES[0]) * HI].rearrange("p (t n) -> p t n", n=HI)
        crow = sb("crow", [P, G * QUARTER], bf16)
        ccol = sb("ccol", [P, G * 32], bf16)
        x0_t = sb("x0_t", [P, HI])
        x1_t = sb("x1_t", [P, HI])
        h_t = sb("h_t", [P, HI])
        rc_t = sb("rc_t", [P, HI])
        y_t = sb("y_t", [P, HI])
        d_t = sb("d_t", [P, HI])
        sq_t = sb("sq_t", [P, HI])
        std_t = sb("std_t", [P, HI])
        out_t = sb("out_t", [P, HI])
        agg_t = sb("agg_t", [P, HI])
        agl_t = sb("agl_t", [P, HI])
        us_t = sb("us_t", [P, HI])
        agg_n = sb("agg_n", [QUARTER, 4 * P])
        tab_rest = agg_n
        u_n = sb("u_n", [QUARTER, 4 * P])
        us_n = sb("us_n", [QUARTER, 4 * P])
        rc_s = sb("rc_s", [QUARTER, 32])
        rc_n = sb("rc_n", [QUARTER, 4 * P])
        tab_n = sb("tab_n", [QUARTER, 4 * P])

        w_ps = [pb(f"w_ps{h}", [P, HALF * FF]) for h in range(2)]
        acc = pb("acc", [P, 512])
        cnt = pb("cnt", [P, 512])
        q0 = pb("q0", [P, 512])
        q1 = pb("q1", [P, 512])

        names = """gathers_begun loads loads_late idx_dst_in zeroed prep idx_ready prod_done red_done
            silu_done s_ready oh_dve oh_act dist_done w_done scat_done cnt_oh cnt_mm wsplit high sub1 mid
            sub2 ys_in y_high y_sub1 y_mid y_sub2 y_out table_written
            w_copied pass_done agg_ready agl_mm agl_ready aggn_tr aggn_ready tp_mm tp_prod tp_red
            us_ready us_tr ust_ready upd_mm y_ready mean_mm d_ready sq_ready var_mm std_ready
            rstd_ready ln_ready h_ready h_tr tab_ready rc_chain rcn_tr rct_ready root_mm
            scaled out_done hi_ready hi_out hi_in cols_made cols_out fetch_mm pick_prod picked
            tab_high tab_sub1 tab_mid parts_ready"""
        S = {n: sem(n) for n in names.split()}
        chunk_in = [sem(f"chunk_in{b}") for b in range(2)]
        chunk_out = [sem(f"chunk_out{b}") for b in range(2)]
        gathered = [[sem(f"gathered{b}{h}") for h in range(2)] for b in range(2)]
        ea_in = [sem(f"ea_in{b}") for b in range(2)]
        cols_in = [sem(f"cols_in{b}") for b in range(2)]

        block = ctx.enter_context(nc.Block())
        early = (
            (idx["src"][:], src_i), (iota[:], iota_d), (wsel[:, 0:3], w_sel0), (wsel[:, 3:6], w_sel), (wraw[:, 0:FF], w0_rep),
            (last_i[:], src_last), (column_of[:], column_d),
        )
        late = (
            (ident[:], ident_d), (avg[:], avg_d), (bdm[:], bd_msg), (bdu[:], bd_upd), (bdt[:], bd_tp),
            (bdr[:, 0, :], bd_root[0]), (bdr[:, 1, :], bd_root[1]), (bdr[:, 2, :], bd_root[2]),
            (br[:], bias_root), (x0_t[:], x_t), (wraw[:, FF:2 * FF], w_rep[0]),
            (wraw[:, 2 * FF:3 * FF], w_rep[1]), (wraw[:, 3 * FF:4 * FF], w_rep[2]),
        )
        EARLY, LATE = 16 * len(early), 16 * len(late)

        @block.sync
        def _(sp):
            def load_chunk(c):
                if c >= 2:
                    sp.wait_ge(S["sub2"], c - 1)
                sp.dma_start(xs[:, c % 2, :], ea0[:, c * CH0:(c + 1) * CH0]).then_inc(chunk_in[c % 2], 16)

            def store_parts(parts, high, mid, low, k, width, done):
                rows = parts.shape[0] // 6
                for n, part in enumerate((high, high, high, mid, mid, low)):
                    view = parts[n * rows:(n + 1) * rows, :].rearrange("i (q c) -> (i q) c", q=P // rows)
                    sp.dma_start(view[:, bass.ds(k * width, width)], part).then_inc(done, 16)

            sp.sem_inc(S["y_out"], 96)
            sp.sem_inc(S["cols_out"], 16)
            sp.dma_start(idx["dst"][:], dst_i).then_inc(S["idx_dst_in"], 16)
            load_chunk(0)
            load_chunk(1)
            for dst, src in early:
                sp.dma_start(dst, src).then_inc(S["loads"], 16)
            for c in range(CHUNKS0):
                sp.wait_ge(S["sub2"], c + 1)
                b = c % 2
                store_parts(parts0, xh[:, b, :], xm[:, b, :], xl[:, b, :], c, CH0, chunk_out[b])
                if c + 2 < CHUNKS0:
                    load_chunk(c + 2)
            sp.dma_start(ys[:], ea1[:, 0:CH1]).then_inc(S["ys_in"], 16)
            for dst, src in late:
                sp.dma_start(dst, src).then_inc(S["loads_late"], 16)
            for b in range(2):
                sp.wait_ge(chunk_out[b], 96 * (CHUNKS0 // 2))
            sp.wait_ge(S["zeroed"], 1)
            sp.wait_ge(S["hi_ready"], 1)
            sp.dma_start(hi_rows, last_hi[:]).then_inc(S["hi_out"], 16)
            sp.wait_ge(S["hi_out"], 16)
            hi_line = hi_rows.rearrange("g e -> (g e)").unsqueeze(0)
            sp.dma_start(hi_all[:], hi_line[:, 0:2 * P].broadcast_to([QUARTER, 2 * P])).then_inc(S["hi_in"], 16)

            def load_group(parts, rows, g, local, b):
                sp.wait_ge(S["w_done"], upto(g, 2, 0) - 2)
                sp.dma_start(ea[0:rows, b, :], parts[:, bass.ds(local * (G * P), G * P)]).then_inc(ea_in[b], 16)

            with sp.Fori(0, ROUNDS) as i:
                for b in range(2):
                    load_group(parts0, ROWS0, i * 2 + b, i * 2 + b, b)
                sp.wait_ge(S["cols_made"], i + 1)
                sp.dma_start(columns[:, bass.ds(i * 8 * P, 8 * P)], cols_new[:].rearrange("p b c e -> p (b c e)")
                             ).then_inc(S["cols_out"], 16)
                sp.dma_start(hi_all[:], hi_line[:, bass.ds(i * 2 * P + 2 * P, 2 * P)].broadcast_to([QUARTER, 2 * P])
                             ).then_inc(S["hi_in"], 16)
                sp.wait_ge(S["y_sub2"], i + 1)
                store_parts(parts1, yh[:], ym[:], yl[:], i, CH1, S["y_out"])
                sp.dma_start(ys[:], ea1[:, bass.ds(i * CH1 + CH1, CH1)]).then_inc(S["ys_in"], 16)
            sp.wait_ge(S["y_out"], 96 * ROUNDS + 96)
            sp.wait_ge(S["cols_out"], 16 * ROUNDS + 16)
            sp.wait_ge(S["ys_in"], 16 * ROUNDS + 16)
            sp.wait_ge(S["hi_in"], 16 * ROUNDS + 16)
            with sp.Fori(0, LAYERS) as l:
                with sp.Fori(0, ROUNDS) as i:
                    for b in range(2):
                        load_group(parts1, ROWS, l * GROUPS + i * 2 + (GROUPS + b), i * 2 + b, b)
                        sp.wait_ge(S["fetch_mm"], upto(l * GROUPS + i * 2 + b, 1, 0) - 1)
                        sp.dma_start(cols_now[:, b, :], columns[:, bass.ds((i * 2 + b) * (4 * P), 4 * P)]
                                     ).then_inc(cols_in[b], 16)
                sp.wait_ge(S["tab_ready"], l + 2)
                sp.dma_start(table.rearrange("(p n) f -> p (n f)", n=32), tab_n[:]).then_inc(S["table_written"], 16)
            sp.wait_ge(S["ln_ready"], 2)
            sp.dma_start(out, out_t[:]).then_inc(S["out_done"], 16)
            sp.wait_ge(S["table_written"], 16 * (LAYERS + 1))
            sp.wait_ge(S["out_done"], 16)

        @block.gpsimd
        def _(pool):
            def gather_group(rows, g, turn, b, tiles):
                for h in range(2):
                    if h == 0:
                        pool.wait_ge(S["idx_ready"], turn)
                    pool.wait_ge(S["prod_done"], upto(g, 2, h + 1) - 4)
                    pool.sem_inc(S["gathers_begun"], 1)
                    for t in range(h * HALF, min((h + 1) * HALF, tiles)):
                        pool.indirect_dma_start(
                            out=xg[:, b, t * F:(t + 1) * F], out_offset=None, in_=rows,
                            in_offset=bass.IndirectOffsetOnAxis(ap=idx_now[:, b, t:t + 1], axis=0),
                        ).then_inc(gathered[b][h], 16)

            with pool.Fori(0, ROUNDS) as i:
                for b in range(2):
                    gather_group(x_rows, i * 2 + b, i * 2 + (b + 1), b, G)
            with pool.Fori(0, LAYERS) as l:
                with pool.Fori(0, ROUNDS) as i:
                    pool.wait_ge(S["table_written"], l * 16 + 16)
                    for b in range(2):
                        gather_group(table, l * GROUPS + i * 2 + (GROUPS + b), l * (GROUPS + 2) + i * 2 + (GROUPS + 2 + b + 1), b,
                                     FETCHED)

        @block.vector
        def _(dve):
            for n, k in (("prod_done", 4), ("red_done", 4), ("s_ready", 4), ("oh_dve", 2), ("cnt_oh", 2), ("picked", 2)):
                dve.sem_inc(S[n], k)
            nc.vector.memset(ea[:], 0.0).then_inc(S["prep"], 1)
            nc.vector.memset(zeros[:], 0.0)
            nc.vector.memset(eps[:], EPS)
            dve.wait_ge(S["prep"], 1)
            nc.vector.memset(ea[96:KROWS, :, :], 1.0).then_inc(S["zeroed"], 1)
            for c in range(CHUNKS0):
                b = c % 2
                dve.wait_ge(S["high"], c + 1)
                nc.vector.tensor_tensor(xs[:, b, :], xs[:, b, :], xh[:, b, :], ALU.subtract).then_inc(S["sub1"], 1)
                dve.wait_ge(S["mid"], c + 1)
                if c >= 2:
                    dve.wait_ge(chunk_out[b], 96 * (c // 2))
                nc.vector.tensor_tensor(xl[:, b, :], xs[:, b, :], xm[:, b, :], ALU.subtract).then_inc(S["sub2"], 1)
            dve.wait_ge(S["loads"], EARLY)
            dve.wait_ge(S["idx_dst_in"], 16)
            made = [1]

            def link(ins):
                made[0] += 1
                ins.then_inc(S["prep"], 1)
                dve.wait_ge(S["prep"], made[0])

            def split_weights(a, b_, k):
                link(nc.vector.tensor_copy(whi[:, a:b_], wraw[:, a:b_]))
                link(nc.vector.tensor_tensor(wres[:, a:b_], wraw[:, a:b_], whi[:, a:b_], ALU.subtract))
                link(nc.vector.tensor_copy(wmid[:, a:b_], wres[:, a:b_]))
                link(nc.vector.tensor_tensor(wlow[:, a:b_], wres[:, a:b_], wmid[:, a:b_], ALU.subtract))
                link(nc.vector.tensor_scalar(wpart[:, a:b_], whi[:, a:b_], wsel[:, k:k + 1], None, ALU.mult))
                for part, j in ((wmid, 1), (wlow, 2)):
                    link(nc.vector.scalar_tensor_tensor(out=wpart[:, a:b_], in0=part[:, a:b_], scalar=wsel[:, k + j:k + j + 1],
                                                        in1=wpart[:, a:b_], op0=ALU.mult, op1=ALU.add))

            link(nc.vector.tensor_scalar(last_i[:], last_i[:], 3, None, ALU.arith_shift_right))
            link(nc.vector.tensor_copy(last_hi[:], last_i[:]))
            dve.sem_inc(S["hi_ready"], 1)
            split_weights(0, FF, 0)
            nc.vector.tensor_copy(w_now[:], wpart[:, 0:FF]).then_inc(S["wsplit"], 1)
            iota_lo = iota[:, 0:LO].unsqueeze(1).broadcast_to([P, TILES, LO])
            for k in ("src", "dst"):
                link(nc.vector.tensor_scalar(tmp_i[:], idx[k][:, 0:TILES], 3, None, ALU.arith_shift_right))
                link(nc.vector.tensor_copy(hi_f[k][:], tmp_i[:]))
                link(nc.vector.tensor_scalar(neg_hi[k][:], hi_f[k][:], -1.0, None, ALU.mult))
                link(nc.vector.tensor_scalar(tmp_i[:], idx[k][:, 0:TILES], LO - 1, None, ALU.bitwise_and))
                link(nc.vector.tensor_copy(lo_f[:], tmp_i[:]))
                link(nc.vector.tensor_tensor(mask[k][:].rearrange("p (t a) -> p t a", a=LO),
                                             lo_f[:].unsqueeze(2).broadcast_to([P, TILES, LO]), iota_lo, ALU.is_equal))
            link(nc.vector.tensor_scalar(tmp_i[:], idx["dst"][:, 0:TILES], 5, None, ALU.arith_shift_right))
            link(nc.vector.tensor_copy(row_f[:], tmp_i[:]))
            link(nc.vector.tensor_scalar(tmp_i[:], idx["dst"][:, 0:TILES], 31, None, ALU.bitwise_and))
            link(nc.vector.tensor_copy(col_f[:], tmp_i[:]))

            assert made[0] == PREP_STEPS

            def products(g, u, b, h, relu):
                dve.wait_ge(gathered[b][h], gathers_done(u, h, relu))
                if relu and h == 1:
                    dve.wait_ge(S["picked"], upto(g - GROUPS, 1, 1))
                dve.wait_ge(S["w_done"], upto(g, 2, h + 1))
                dve.wait_ge(S["red_done"], upto(g, 2, h + 1) - 2)
                w = w_ps[h][:].rearrange("p (i o) -> p i o", o=F)
                xin = xg[:, b, h * HALF * F:(h + 1) * HALF * F].unsqueeze(2).broadcast_to([P, HALF * F, F])
                o = prod[:, h, :].rearrange("p (i o) -> p i o", o=F)
                if relu:
                    ins = nc.vector.scalar_tensor_tensor(out=o, in0=w, scalar=0.0, in1=xin, op0=ALU.max, op1=ALU.mult)
                else:
                    ins = nc.vector.tensor_tensor(o, w, xin, ALU.mult)
                ins.then_inc(S["prod_done"], 1)

            def reduce_half(g, b, h, free):
                dve.wait_ge(S["prod_done"], upto(g, 2, h + 1))
                dve.wait_ge(free, upto(g, 2, h + 1) - 4)
                nc.vector.tensor_reduce(
                    out=msg[:, b, h * HALF * F:(h + 1) * HALF * F].rearrange("p (t o) -> p t o", o=F),
                    in_=prod[:, h, :].rearrange("p (t i o) -> p t o i", i=F, o=F), axis=AX.X, op=ALU.add,
                ).then_inc(S["red_done"], 1)

            def one_hots(g, local, b, which, tiles):
                dve.wait_ge(S["scat_done"], upto(g, 1, 0) - 1)
                for t in tiles:
                    ins = nc.vector.tensor_scalar(onehot[:, b, t, :], iota[:], hi_f[which][:, bass.ds(local * G + t, 1)],
                                                  None, ALU.is_equal)
                ins.then_inc(S["oh_dve"], 1)

            def spread_half(g, local, b, h, which, source, ready):
                dve.wait_ge(ready, upto(g, 2, h + 1))
                nc.vector.tensor_tensor(
                    spread[:, b, h * HALF * P:(h + 1) * HALF * P].rearrange("p (t a o) -> p t a o", a=LO, o=F),
                    mask[which][:, bass.ds(local * (G * LO) + h * HALF * LO, HALF * LO)].rearrange("p (t a) -> p t a", a=LO)
                    .unsqueeze(3).broadcast_to([P, HALF, LO, F]),
                    source[:, b, h * HALF * F:(h + 1) * HALF * F].rearrange("p (t o) -> p t o", o=F)
                    .unsqueeze(2).broadcast_to([P, HALF, LO, F]),
                    ALU.mult).then_inc(S["s_ready"], 1)

            def pick(g, local, b):
                dve.wait_ge(S["fetch_mm"], upto(g - GROUPS, 1, 1))
                dve.wait_ge(S["picked"], upto(g - GROUPS, 1, 0))
                nc.vector.tensor_tensor(
                    picks[:].rearrange("p (a f) -> p a f", f=F), cnt[:, b * P:(b + 1) * P].rearrange("p (a f) -> p a f", f=F),
                    mask["src"][:, bass.ds(local * (G * LO) + FETCHED * LO, LO)].unsqueeze(2).broadcast_to([P, LO, F]),
                    ALU.mult).then_inc(S["pick_prod"], 1)

            def sum_picks(g, b):
                dve.wait_ge(S["pick_prod"], g - (GROUPS - 1))
                dve.wait_ge(S["prod_done"], upto(g, 2, 2) - 4)
                nc.vector.tensor_reduce(out=xg[:, b, FETCHED * F:G * F], in_=picks[:].rearrange("p (a f) -> p f a", f=F),
                                        axis=AX.X, op=ALU.add).then_inc(S["picked"], 1)

            def group(g, u, local, b, which, first_pass):
                free = S["silu_done"] if first_pass else S["s_ready"]
                tiles = [t for t in range(G) if t not in ACT_TILES[0 if first_pass else 1]]
                one_hots(g, local, b, which, tiles)
                if first_pass and b == 0:
                    dve.wait_ge(S["y_high"], u + 1)
                    nc.vector.tensor_tensor(ys[:], ys[:], yh[:], ALU.subtract).then_inc(S["y_sub1"], 1)
                    dve.wait_ge(S["hi_in"], u * 16 + 16)
                    dve.wait_ge(S["cols_out"], u * 16 + 16)
                    for c in range(4):
                        ins = nc.vector.tensor_scalar(cols_new[:, :, c, :], hi_all[:].rearrange("p (b e) -> p b e", e=P),
                                                      column_of[:, c:c + 1], None, ALU.is_equal)
                    ins.then_inc(S["cols_made"], 1)
                if not first_pass:
                    pick(g, local, b)
                products(g, u, b, 0, not first_pass)
                if not first_pass:
                    sum_picks(g, b)
                products(g, u, b, 1, not first_pass)
                reduce_half(g, b, 0, free)
                reduce_half(g, b, 1, free)
                if first_pass:
                    if b == 0:
                        dve.wait_ge(S["y_mid"], u + 1)
                        nc.vector.tensor_tensor(yl[:], ys[:], ym[:], ALU.subtract).then_inc(S["y_sub2"], 1)
                    dve.wait_ge(S["cnt_mm"], g + 1)
                    for o, f, w in ((crow, row_f, QUARTER), (ccol, col_f, 32)):
                        ins = nc.vector.tensor_tensor(
                            o[:].rearrange("p (t w) -> p t w", w=w),
                            f[:, bass.ds(local * G, G)].unsqueeze(2).broadcast_to([P, G, w]),
                            iota[:, 0:w].unsqueeze(1).broadcast_to([P, G, w]), ALU.is_equal)
                    ins.then_inc(S["cnt_oh"], 1)
                for h in range(2):
                    spread_half(g, local, b, h, which, act_msg if first_pass else msg,
                                S["silu_done"] if first_pass else S["red_done"])

            with dve.Fori(0, ROUNDS) as i:
                for b in range(2):
                    group(i * 2 + b, i, i * 2 + b, b, "src", True)

            dve.wait_ge(S["loads_late"], LATE)
            split_weights(FF, (LAYERS + 1) * FF, 3)
            dve.wait_ge(S["pass_done"], 1)
            nc.vector.tensor_scalar(rc_s[:], cnt[0:QUARTER, 0:32], 1.0, None, ALU.max).then_inc(S["rc_chain"], 1)
            dve.wait_ge(S["rc_chain"], 1)
            nc.vector.reciprocal(rc_s[:], rc_s[:]).then_inc(S["rc_chain"], 1)
            dve.wait_ge(S["rc_chain"], 2)
            nc.vector.tensor_copy(rc_n[:].rearrange("p (m f) -> p m f", f=F),
                                  rc_s[:].unsqueeze(2).broadcast_to([QUARTER, 32, F])).then_inc(S["rc_chain"], 1)

            dve.wait_ge(S["aggn_ready"], 1)
            for k in range(8):
                h = k % 2
                dve.wait_ge(S["tp_mm"], k + 1)
                if k >= 2:
                    dve.wait_ge(S["tp_red"], k - 1)
                nc.vector.tensor_tensor(
                    prod[0:QUARTER, h, :].rearrange("p (i o) -> p i o", o=F),
                    w_ps[h][0:QUARTER, :].rearrange("p (i o) -> p i o", o=F),
                    agg_n[:, k * HALF * F:(k + 1) * HALF * F].unsqueeze(2).broadcast_to([QUARTER, HALF * F, F]),
                    ALU.mult).then_inc(S["tp_prod"], 1)
                dve.wait_ge(S["tp_prod"], k + 1)
                nc.vector.tensor_reduce(
                    out=u_n[:, k * HALF * F:(k + 1) * HALF * F].rearrange("p (t o) -> p t o", o=F),
                    in_=prod[0:QUARTER, h, :].rearrange("p (t i o) -> p t o i", i=F, o=F), axis=AX.X,
                    op=ALU.add).then_inc(S["tp_red"], 1)
            dve.wait_ge(S["upd_mm"], 1)
            nc.vector.scalar_tensor_tensor(out=y_t[:], in0=q0[:, 0:HI], scalar=NORM_LIN, in1=x0_t[:],
                                           op0=ALU.mult, op1=ALU.add).then_inc(S["scaled"], 1)
            dve.wait_ge(S["scaled"], 1)
            nc.vector.tensor_tensor(y_t[:], y_t[:], x0_t[:], ALU.add).then_inc(S["y_ready"], 1)

            def layer_norm(n, to):
                dve.wait_ge(S["mean_mm"], n)
                nc.vector.tensor_tensor(d_t[:], y_t[:], q0[:, 0:HI], ALU.subtract).then_inc(S["d_ready"], 1)
                dve.wait_ge(S["std_ready"], n)
                nc.vector.reciprocal(std_t[:], std_t[:]).then_inc(S["rstd_ready"], 1)
                dve.wait_ge(S["rstd_ready"], n)
                nc.vector.tensor_tensor(to[:], d_t[:], std_t[:], ALU.mult).then_inc(S["ln_ready"], 1)

            layer_norm(1, x1_t)
            dve.wait_ge(S["ln_ready"], 1)
            nc.vector.tensor_copy(h_t[:], x1_t[:]).then_inc(S["h_ready"], 1)

            with dve.Fori(0, LAYERS) as l:
                dve.wait_ge(S["tab_high"], l + 1)
                nc.vector.tensor_tensor(tab_rest[:], tab_n[:], tab_parts[:, 0, :], ALU.subtract).then_inc(S["tab_sub1"], 1)
                dve.wait_ge(S["tab_mid"], l + 1)
                nc.vector.tensor_tensor(tab_parts[:, 2, :], tab_rest[:], tab_parts[:, 1, :], ALU.subtract
                                        ).then_inc(S["parts_ready"], 1)
                with dve.Fori(0, ROUNDS) as i:
                    for b in range(2):
                        group(l * GROUPS + i * 2 + (GROUPS + b), l * ROUNDS + i + ROUNDS, i * 2 + b, b, "dst", False)
                dve.wait_ge(S["rct_ready"], 1)
                dve.wait_ge(S["root_mm"], l + 1)
                nc.vector.tensor_tensor(y_t[:], acc[:, 0:HI], rc_t[:], ALU.mult).then_inc(S["scaled"], 1)
                dve.wait_ge(S["scaled"], l + 2)
                nc.vector.scalar_tensor_tensor(out=h_t[:], in0=q0[:, 0:HI], scalar=br_now[:], in1=y_t[:],
                                               op0=ALU.add, op1=ALU.add).then_inc(S["h_ready"], 1)
            dve.wait_ge(S["h_ready"], LAYERS + 1)
            nc.vector.tensor_tensor(y_t[:], h_t[:], x1_t[:], ALU.add).then_inc(S["y_ready"], 1)
            layer_norm(2, out_t)

        @block.scalar
        def _(act):
            for n, k in (("oh_act", 2), ("silu_done", 4)):
                act.sem_inc(S[n], k)

            def copy_indices(which, local, b):
                nc.scalar.activation(idx_now[:, b, :], idx[which][:, bass.ds(local * G, G)], ACT.Copy).then_inc(S["idx_ready"], 1)

            act.wait_ge(S["idx_dst_in"], 16)
            for b in range(2):
                copy_indices("dst", b, b)
            for c in range(CHUNKS0):
                b = c % 2
                act.wait_ge(chunk_in[b], 16 * (c // 2 + 1))
                if c >= 2:
                    act.wait_ge(chunk_out[b], 96 * (c // 2))
                nc.scalar.activation(xh[:, b, :], xs[:, b, :], ACT.Copy).then_inc(S["high"], 1)
                act.wait_ge(S["sub1"], c + 1)
                nc.scalar.activation(xm[:, b, :], xs[:, b, :], ACT.Copy).then_inc(S["mid"], 1)
            act.wait_ge(S["loads"], EARLY)
            act.wait_ge(S["prep"], PREP_STEPS)

            def one_hots(g, before, local, b, which, tiles, between=None):
                act.wait_ge(S["oh_act"], upto(g, 1, 0))
                act.wait_ge(S["loads"], EARLY)
                for j, t in enumerate(tiles):
                    nc.scalar.activation(dist[:, j, :], iota[:], ACT.Abs,
                                         bias=neg_hi[which][:, bass.ds(local * G + t, 1)]).then_inc(S["dist_done"], 1)
                if between:
                    between()
                act.wait_ge(S["scat_done"], upto(g, 1, 0) - 1)
                for j, t in enumerate(tiles):
                    act.wait_ge(S["dist_done"], before + (j + 1))
                    ins = nc.scalar.activation(onehot[:, b, t, :], dist[:, j, :], ACT.Relu, scale=-1.0, bias=1.0)
                ins.then_inc(S["oh_act"], 1)

            def silu_half(g, b, h):
                act.wait_ge(S["red_done"], upto(g, 2, h + 1))
                act.wait_ge(S["s_ready"], upto(g, 2, h + 1) - 4)
                nc.scalar.activation(act_msg[:, b, h * HALF * F:(h + 1) * HALF * F], msg[:, b, h * HALF * F:(h + 1) * HALF * F],
                                     ACT.Silu, scale=NORM_MSG).then_inc(S["silu_done"], 1)

            def next_indices(which, u, local, b, layers):
                for h in range(2):
                    act.wait_ge(gathered[b][h], gathers_done(u, h, layers))
                act.wait_ge(S["idx_dst_in"], 16)
                copy_indices(which, local + 2, b)

            n0, n1 = map(len, ACT_TILES)
            with act.Fori(0, ROUNDS) as i:
                for b in range(2):
                    between = None
                    if b == 0:
                        act.wait_ge(S["ys_in"], i * 16 + 16)
                        act.wait_ge(S["y_out"], i * 96 + 96)
                        nc.scalar.activation(yh[:], ys[:], ACT.Copy).then_inc(S["y_high"], 1)

                        def between():
                            act.wait_ge(S["y_sub1"], i + 1)
                            nc.scalar.activation(ym[:], ys[:], ACT.Copy).then_inc(S["y_mid"], 1)

                    one_hots(i * 2 + b, (i * 2 + b) * n0, i * 2 + b, b, "src", ACT_TILES[0], between)
                    next_indices("dst", i, i * 2 + b, b, False)
                    for h in range(2):
                        silu_half(i * 2 + b, b, h)

            act.wait_ge(S["pass_done"], 1)
            nc.scalar.activation(agg_t[:], acc[:, 0:HI], ACT.Copy).then_inc(S["agg_ready"], 1)
            act.wait_ge(S["agl_mm"], 1)
            nc.scalar.activation(agl_t[:], q0[:, 0:HI], ACT.Copy, scale=NORM_LIN).then_inc(S["agl_ready"], 1)
            act.wait_ge(S["aggn_tr"], 1)
            nc.scalar.activation(agg_n[:], q1[0:QUARTER, :], ACT.Copy).then_inc(S["aggn_ready"], 1)
            act.wait_ge(S["rcn_tr"], 1)
            nc.scalar.activation(rc_t[:].rearrange("q (p c) -> q c p", c=4),
                                 q0[:, 0:HI].rearrange("q (c p) -> q c p", c=4), ACT.Copy).then_inc(S["rct_ready"], 1)
            act.wait_ge(S["tp_red"], 8)
            nc.scalar.activation(us_n[:], u_n[:], ACT.Silu, scale=NORM_UPD).then_inc(S["us_ready"], 1)
            act.wait_ge(S["us_tr"], 1)
            nc.scalar.activation(us_t[:].rearrange("q (p c) -> q c p", c=4),
                                 q1[:, 0:HI].rearrange("q (c p) -> q c p", c=4), ACT.Copy).then_inc(S["ust_ready"], 1)

            def layer_norm(n):
                act.wait_ge(S["d_ready"], n)
                nc.scalar.activation(sq_t[:], d_t[:], ACT.Square).then_inc(S["sq_ready"], 1)
                act.wait_ge(S["var_mm"], n)
                nc.scalar.activation(std_t[:], q1[:, 0:HI], ACT.Sqrt, bias=eps[:]).then_inc(S["std_ready"], 1)

            layer_norm(1)
            act.wait_ge(S["h_tr"], 1)
            nc.scalar.activation(tab_n[:], q1[0:QUARTER, :], ACT.Copy).then_inc(S["tab_ready"], 1)
            act.wait_ge(S["tab_ready"], 1)
            act.dma_start(table.rearrange("(p n) f -> p (n f)", n=32), tab_n[:]).then_inc(S["table_written"], 16)

            with act.Fori(0, LAYERS) as l:
                act.wait_ge(S["idx_ready"], l * (GROUPS + 2) + (GROUPS + 2))
                for b in range(2):
                    copy_indices("src", b, b)
                act.wait_ge(S["tab_ready"], l + 1)
                nc.scalar.activation(tab_parts[:, 0, :], tab_n[:], ACT.Copy).then_inc(S["tab_high"], 1)
                act.wait_ge(S["h_ready"], l + 1)
                act.wait_ge(S["loads"], EARLY)
                nc.scalar.activation(w_now[:], wpart[:, bass.ds(l * FF + FF, FF)], ACT.Copy)
                nc.scalar.activation(bdr_now[:], bdr[:].rearrange("p l c -> p (l c)")[:, bass.ds(l * P, P)], ACT.Copy)
                nc.scalar.activation(br_now[:], br[:, bass.ds(l, 1)], ACT.Copy).then_inc(S["w_copied"], 1)
                act.wait_ge(S["tab_sub1"], l + 1)
                nc.scalar.activation(tab_parts[:, 1, :], tab_rest[:], ACT.Copy).then_inc(S["tab_mid"], 1)
                with act.Fori(0, ROUNDS) as i:
                    for b in range(2):
                        one_hots(l * GROUPS + i * 2 + (GROUPS + b), (l * GROUPS + i * 2 + b) * n1 + GROUPS * n0,
                                 i * 2 + b, b, "dst", ACT_TILES[1])
                        next_indices("src", l * ROUNDS + i + ROUNDS, i * 2 + b, b, True)
                act.wait_ge(S["h_tr"], l + 2)
                act.wait_ge(S["table_written"], l * 16 + 16)
                nc.scalar.activation(tab_n[:], q1[0:QUARTER, :], ACT.Copy).then_inc(S["tab_ready"], 1)
            layer_norm(2)

        @block.tensor
        def _(pe):
            for n, k in (("w_done", 4), ("scat_done", 2), ("cnt_mm", 1), ("fetch_mm", 2)):
                pe.sem_inc(S[n], k)
            pe.wait_ge(S["wsplit"], 1)

            def weights(g, u, b):
                pe.wait_ge(ea_in[b], u * 16 + 16)
                for h in range(2):
                    pe.wait_ge(S["prod_done"], upto(g, 2, h + 1) - 2)
                    for j in range(HALF):
                        t = h * HALF + j
                        last = nc.tensor.matmul(w_ps[h][:, j * FF:(j + 1) * FF], ea[:, b, t * P:(t + 1) * P],
                                                w_now[:], start=True, stop=True)
                    last.then_inc(S["w_done"], 1)

            def fetch(g, u, b):
                pe.wait_ge(cols_in[b], (u - ROUNDS) * 16 + 16)
                pe.wait_ge(S["picked"], upto(g - GROUPS, 1, 0) - 1)
                for c in range(4):
                    for part in range(3):
                        last = nc.tensor.matmul(cnt[:, b * P:(b + 1) * P], cols_now[:, b, c * P:(c + 1) * P],
                                                tab_parts[:, part, c * P:(c + 1) * P], start=c + part == 0,
                                                stop=c + part == 5)
                last.then_inc(S["fetch_mm"], 1)

            def prepare(g, u, b, first_pass):
                weights(g, u, b)
                if not first_pass:
                    fetch(g, u, b)

            def scatter(g, b, counts):
                if counts:
                    pe.wait_ge(S["cnt_oh"], upto(g, 1, 1))
                    for t in range(G):
                        last = nc.tensor.matmul(cnt[0:QUARTER, 0:32], crow[:, t * QUARTER:(t + 1) * QUARTER],
                                                ccol[:, t * 32:(t + 1) * 32], start=False, stop=False)
                    last.then_inc(S["cnt_mm"], 1)
                pe.wait_ge(S["oh_dve"], upto(g, 1, 1))
                pe.wait_ge(S["oh_act"], upto(g, 1, 1))
                for h in range(2):
                    pe.wait_ge(S["s_ready"], upto(g, 2, h + 1))
                    for t in range(h * HALF, (h + 1) * HALF):
                        last = nc.tensor.matmul(acc[:, 0:HI], spread[:, b, t * P:(t + 1) * P], onehot[:, b, t, :],
                                                start=False, stop=False)
                last.then_inc(S["scat_done"], 1)

            def edge_pass(g0, u0, counts):
                nc.tensor.matmul(acc[:, 0:HI], zeros[:, 0:P], zeros[:, 0:HI], start=True, stop=False)
                if counts:
                    nc.tensor.matmul(cnt[0:QUARTER, 0:32], zeros[:, 0:QUARTER], zeros[:, 0:32], start=True, stop=False)
                prepare(g0, u0, 0, counts)
                with pe.Fori(0, ROUNDS - 1) as i:
                    prepare(i * 2 + g0 + 1, i + u0, 1, counts)
                    scatter(i * 2 + g0, 0, counts)
                    prepare(i * 2 + g0 + 2, i + u0 + 1, 0, counts)
                    scatter(i * 2 + g0 + 1, 1, counts)
                prepare(g0 + (GROUPS - 1), u0 + (ROUNDS - 1), 1, counts)
                scatter(g0 + (GROUPS - 2), 0, counts)
                scatter(g0 + (GROUPS - 1), 1, counts)
                if counts:
                    nc.tensor.matmul(cnt[0:QUARTER, 0:32], zeros[:, 0:QUARTER], zeros[:, 0:32], start=False, stop=True)
                nc.tensor.matmul(acc[:, 0:HI], zeros[:, 0:P], zeros[:, 0:HI], start=False,
                                 stop=True).then_inc(S["pass_done"], 1)

            def to_rows(of, done):
                view = of[:].rearrange("q (p c) -> q c p", c=4)
                for c in range(4):
                    last = nc.tensor.transpose(q1[0:QUARTER, c * P:(c + 1) * P], view[:, c, :], ident[:])
                last.then_inc(done, 1)

            def to_columns(to, of, done):
                for c in range(4):
                    last = nc.tensor.transpose(to[:, c * QUARTER:(c + 1) * QUARTER], of[:, c * P:(c + 1) * P],
                                               ident[0:QUARTER, 0:QUARTER])
                last.then_inc(done, 1)

            def layer_norm(n):
                pe.wait_ge(S["y_ready"], n)
                nc.tensor.matmul(q0[:, 0:HI], avg[:], y_t[:], start=True, stop=True).then_inc(S["mean_mm"], 1)
                pe.wait_ge(S["sq_ready"], n)
                nc.tensor.matmul(q1[:, 0:HI], avg[:], sq_t[:], start=True, stop=True).then_inc(S["var_mm"], 1)

            x_view = x0_t[:].rearrange("q (p c) -> q c p", c=4)

            def transform(k):
                h = k % 2
                if k >= 2:
                    pe.wait_ge(S["tp_prod"], k - 1)
                for j in range(2):
                    at = h * HALF * FF + j * 512
                    last = nc.tensor.matmul(w_ps[h][0:QUARTER, j * 512:(j + 1) * 512], x_view[:, k // 2, :],
                                            bdt[:, at:at + 512], start=True, stop=True)
                last.then_inc(S["tp_mm"], 1)

            edge_pass(0, 0, True)
            pe.wait_ge(S["loads_late"], LATE)
            pe.wait_ge(S["prod_done"], upto(GROUPS - 1, 2, 2))
            transform(0)
            transform(1)
            pe.wait_ge(S["agg_ready"], 1)
            nc.tensor.matmul(q0[:, 0:HI], bdm[:], agg_t[:], start=True, stop=True).then_inc(S["agl_mm"], 1)
            pe.wait_ge(S["agl_ready"], 1)
            to_rows(agl_t, S["aggn_tr"])
            for k in range(2, 8):
                transform(k)
            pe.wait_ge(S["rc_chain"], 3)
            to_columns(q0, rc_n, S["rcn_tr"])
            pe.wait_ge(S["us_ready"], 1)
            to_columns(q1, us_n, S["us_tr"])
            pe.wait_ge(S["ust_ready"], 1)
            pe.wait_ge(S["rct_ready"], 1)
            nc.tensor.matmul(q0[:, 0:HI], bdu[:], us_t[:], start=True, stop=True).then_inc(S["upd_mm"], 1)
            layer_norm(1)
            pe.wait_ge(S["h_ready"], 1)
            to_rows(h_t, S["h_tr"])

            with pe.Fori(0, LAYERS) as l:
                pe.wait_ge(S["w_copied"], l + 1)
                pe.wait_ge(S["parts_ready"], l + 1)
                edge_pass(l * GROUPS + GROUPS, l * ROUNDS + ROUNDS, False)
                nc.tensor.matmul(q0[:, 0:HI], bdr_now[:], h_t[:], start=True, stop=True).then_inc(S["root_mm"], 1)
                pe.wait_ge(S["h_ready"], l + 2)
                to_rows(h_t, S["h_tr"])
            pe.wait_ge(S["tab_ready"], LAYERS + 1)
            layer_norm(2)


def kernel(**inputs):
    import numpy as np
    import concourse.bacc as bacc
    from concourse.bass_utils import run_bass_kernel_spmd as run

    a = {k: np.asarray(v) for k, v in inputs.items()}
    f4 = np.float32

    def blocks(w):
        o = np.zeros((P, LO * w.shape[1]), w.dtype)
        for k in range(LO):
            o[k * F:(k + 1) * F, k * w.shape[1]:(k + 1) * w.shape[1]] = w
        return o

    def rows(w, bias=None):
        o = np.zeros((KROWS, FF), w.dtype)
        for k in range(6):
            o[k * w.shape[0]:(k + 1) * w.shape[0]] = w
        if bias is not None:
            o[96:99] = bias
        return o

    def select(r, bias):
        o = np.zeros((KROWS, 3), f4)
        for k, part in enumerate((0, 1, 2, 0, 1, 0)):
            o[k * r:(k + 1) * r, part] = 1.0
        if bias:
            o[96:99] = np.eye(3, dtype=f4)
        return o

    def indices(v):
        o = np.full(EDGES + 2 * G * P, PAD_NODE, np.int32)
        o[:N_EDGES] = v
        return np.ascontiguousarray(o.reshape(TILES + 2 * G, P).T)

    def flat(v):
        o = np.zeros((v.shape[1], EDGES), v.dtype)
        o[:, :N_EDGES] = v.T
        o = o.reshape(P, -1)
        return np.concatenate([o, np.zeros((P, CH1), v.dtype)], 1)

    x = np.zeros((NODES, F), a["x"].dtype)
    x[:N_NODES] = a["x"]
    tp0 = a["L0_gnn_W_msg_tp"].transpose(1, 0, 2).reshape(F_EDGE0, FF)
    upd = a["L0_gnn_W_upd_tp"].reshape(F, FF)
    layers = ("1", "2", "3")
    arrays = {
        "x_rows": x,
        "x_t": np.ascontiguousarray(x.reshape(HI, LO * F).T),
        "src": indices(a["src"]), "dst": indices(a["dst"]),
        "ea0": flat(a["edge_attr_8"]), "ea1": flat(a["edge_attr_16"]),
        "w0": rows(tp0),
        "w": np.stack([rows(a[f"L1_gnn_Wn{k}"], a[f"L1_gnn_bn{k}"]) for k in layers]),
        "sel0": select(F_EDGE0, False), "sel": select(F, True),
        "bd_msg": blocks(a["L0_gnn_W_msg_lin"]), "bd_upd": blocks(a["L0_gnn_W_upd_lin"]),
        "bd_root": np.stack([blocks(a[f"L1_gnn_Wr{k}"]) for k in layers]),
        "bias_root": np.ascontiguousarray(np.stack([np.tile(a[f"L1_gnn_b{k}"], LO) for k in layers]).T),
        "bd_tp": blocks(upd),
        "ident": np.eye(P, dtype=f4),
        "iota": np.tile(np.arange(HI, dtype=f4), (P, 1)),
        "avg": np.kron(np.eye(LO, dtype=f4), np.full((F, F), 1.0 / F, f4)),
        "src_last": indices(a["src"]).T[FETCHED::G],
        "column": np.arange(HI, dtype=f4).reshape(QUARTER, 4),
    }
    arrays = {f"in_{k}": np.ascontiguousarray(v) for k, v in arrays.items()}
    nc = bacc.Bacc("TRN2", target_bir_lowering=False, num_devices=1)
    args = [nc.dram_tensor(k, v.shape, mybir.dt.from_np(v.dtype), kind="ExternalInput").ap() for k, v in arrays.items()]
    out = nc.dram_tensor("out_nodes", (P, HI), mybir.dt.float32, kind="ExternalOutput").ap()
    gnn_kernel(nc, *args, out)
    got = run(nc, [arrays], core_ids=[0]).results[0]["out_nodes"]
    return np.ascontiguousarray(got.T.reshape(NODES, F)[:N_NODES])
```

```python
import concourse.bass as bass
from concourse import mybir
from contextlib import ExitStack

N_NODES, F = 3125, 16
N_EDGES, F_EDGE0 = 100000, 8
FF = F * F
LAYERS = 3
P = 128
LO = P // F
HI = 392
NODES = LO * HI
QUARTER = HI // 4
G = 8
TILES = 784
EDGES = TILES * P
GROUPS = TILES // G
ROUNDS = GROUPS // 2
HALF = G // 2
PAD_NODE = NODES - 1
ROW_Y = F_EDGE0 * F
ROWS = 6 * F
KROWS = 112
CH1 = EDGES * F // P // ROUNDS
EPS = 1e-5
NORM_MSG = float(1.0 / (F * F_EDGE0) ** 0.5)
NORM_UPD = float(1.0 / (F * F) ** 0.5)
NORM_LIN = float(1.0 / F ** 0.5)
KINDS = ("src", "dst")
FIRST_ACT_TILE = (3, 1)
FETCH_FROM = (7, 7)
N_FETCH = tuple(G - t for t in FETCH_FROM)
SLOT = (0, N_FETCH[0])
SLOTS = sum(N_FETCH)


def upto(g, n, k):
    return (g + 2) * n + k


def gathers_done(u, b, h):
    tiles = HALF if h == 0 else FETCH_FROM[b] - HALF
    return u * (16 * tiles) + 16 * tiles


def gnn_kernel(nc, x_t, src_i, dst_i, ea0, ea1, bd_y_d, w_rep, w_sel, bd_msg, bd_upd,
               bd_root, bias_root, bd_tp, ident_d, iota_d, avg_d, last_d, column_d, x_n, w_y_d, out):
    f32, bf16, f16, i32 = mybir.dt.float32, mybir.dt.bfloat16, mybir.dt.float16, mybir.dt.int32
    ALU, ACT, AX = mybir.AluOpType, mybir.ActivationFunctionType, mybir.AxisListType

    y_table = nc.dram_tensor("y_table", [NODES, ROW_Y], f32, kind="Internal").ap()
    table = nc.dram_tensor("node_table", [NODES, F], f32, kind="Internal").ap()
    parts1 = nc.dram_tensor("edge_parts1", [ROWS, EDGES], bf16, kind="Internal").ap()
    hi_rows = nc.dram_tensor("hi_rows", [ROUNDS + 1, SLOTS, 2, P], f16, kind="Internal").ap()
    lo_rows = nc.dram_tensor("lo_rows", [ROUNDS + 1, SLOTS, P], f16, kind="Internal").ap()
    columns = nc.dram_tensor("one_hot_columns", [QUARTER, (ROUNDS + 1) * SLOTS * 4 * P], bf16, kind="Internal").ap()

    ctx = ExitStack()
    with ctx:
        def sb(name, shape, dt=f32):
            return ctx.enter_context(nc.sbuf_tensor(name, shape, dt))

        def pb(name, shape, dt=f32):
            return ctx.enter_context(nc.psum_tensor(name, shape, dt))

        def sem(name):
            return ctx.enter_context(nc.semaphore(name))

        ident = sb("ident", [P, P])
        iota = sb("iota", [P, HI])
        avg = sb("avg", [P, P])
        zeros = sb("zeros", [P, HI], bf16)
        eps = sb("eps", [P, 1])
        bdm = sb("bdm", [P, P])
        bdu = sb("bdu", [P, P])
        bdr = sb("bdr", [P, LAYERS, P])
        bdr_now = sb("bdr_now", [P, P])
        br = sb("br", [P, LAYERS])
        br_now = sb("br_now", [P, 1])
        bdy = sb("bdy", [P, LO * ROW_Y])
        bdt = sb("bdt", [P, LO * FF])
        wraw = sb("wraw", [KROWS, LAYERS * FF])
        whi = sb("whi", [KROWS, LAYERS * FF], bf16)
        wmid = sb("wmid", [KROWS, LAYERS * FF], bf16)
        wlow = sb("wlow", [KROWS, LAYERS * FF], bf16)
        wpart = sb("wpart", [KROWS, LAYERS * FF], bf16)
        wsel = sb("wsel", [KROWS, 3])
        w_now = sb("w_now", [KROWS, FF], bf16)
        idx = {k: sb("idx_" + k, [P, TILES + 2 * G], i32) for k in ("src", "dst")}
        tmp_i = sb("tmp_i", [P, TILES], i32)
        lo_f = sb("lo_f", [P, 2, TILES], bf16)
        hi_f = {k: sb("hi_" + k, [P, TILES]) for k in ("src", "dst")}
        neg_hi = {k: sb("neg_hi_" + k, [P, TILES]) for k in ("src", "dst")}
        masks = sb("masks", [P, 2, TILES * LO], bf16)
        mask = {k: masks[:, n] for n, k in enumerate(KINDS)}
        row_f = sb("row_f", [P, TILES])
        col_f = sb("col_f", [P, TILES])
        ys = sb("ys", [P, CH1])
        yh = sb("yh", [P, CH1], bf16)
        ym = sb("ym", [P, CH1], bf16)
        yl = sb("yl", [P, CH1], bf16)
        last_i = sb("last_i", [ROUNDS + 1, SLOTS, 2, P], i32)
        last_tmp = tmp_i[0:ROUNDS + 1, 0:SLOTS * 2 * P].rearrange("r (t k e) -> r t k e", t=SLOTS, k=2)
        last_hi = sb("last_hi", [ROUNDS + 1, SLOTS, 2, P], f16)
        last_lo = sb("last_lo", [ROUNDS + 1, SLOTS, P], f16)
        hi_all = sb("hi_all", [QUARTER, SLOTS, 2, P], f16)
        lo_all = sb("lo_all", [P, SLOTS, P], f16)
        column_of = sb("column_of", [P, 5])
        w_y = sb("w_y", [P, ROW_Y])
        x_masked = sb("x_masked", [P, SLOTS, P])
        cols_new = sb("cols_new", [QUARTER, 2, SLOTS, 4, P], bf16)
        cols_now = sb("cols_now", [QUARTER, SLOTS, 4, P], bf16)
        tab_parts = sb("tab_parts", [QUARTER, 3, 4 * P], bf16)
        picks = sb("picks", [P, max(N_FETCH) * P])
        idx_now = sb("idx_now", [P, 2, G], i32)
        xg = sb("xg", [P, 2, G * F])
        yg = sb("yg", [P, 2, G * ROW_Y])
        ea0_now = sb("ea0_now", [P, 2, G * F_EDGE0])
        ea = sb("ea", [KROWS, 2, G * P], bf16)
        prod = sb("prod", [P, 2, HALF * FF])
        msg = sb("msg", [P, 2, G * F])
        act_msg = sb("act_msg", [P, 2, G * F])
        spread = sb("spread", [P, 2, G * P])
        onehot = sb("onehot", [P, 2, G, HI])
        y_n = onehot[0:QUARTER].rearrange("p b t n -> p (b t n)")[:, 0:4 * LO * ROW_Y]
        dist = sb("dist", [P, G - min(FIRST_ACT_TILE), HI])
        crow = sb("crow", [P, G * QUARTER], bf16)
        ccol = sb("ccol", [P, G * 32], bf16)
        x0_t = sb("x0_t", [P, HI])
        x1_t = sb("x1_t", [P, HI])
        h_t = sb("h_t", [P, HI])
        rc_t = sb("rc_t", [P, HI])
        y_t = sb("y_t", [P, HI])
        d_t = sb("d_t", [P, HI])
        sq_t = sb("sq_t", [P, HI])
        std_t = sb("std_t", [P, HI])
        out_t = sb("out_t", [P, HI])
        agg_t = sb("agg_t", [P, HI])
        us_t = sb("us_t", [P, HI])
        agg_n = sb("agg_n", [QUARTER, 4 * P])
        tab_rest = agg_n
        u_n = sb("u_n", [QUARTER, 4 * P])
        us_n = sb("us_n", [QUARTER, 4 * P])
        x2_n = sb("x2_n", [QUARTER, 4 * P])
        v_n, d_n, sq_n = u_n, us_n, agg_n
        sum_n = sb("sum_n", [QUARTER, 32])
        std_n = sb("std_n", [QUARTER, 32])
        rc_s = sb("rc_s", [QUARTER, 32])
        rc_n = sb("rc_n", [QUARTER, 4 * P])
        tab_n = sb("tab_n", [QUARTER, 4 * P])

        w_ps = [pb(f"w_ps{h}", [P, HALF * FF]) for h in range(2)]
        acc = pb("acc", [P, 512])
        cnt = pb("cnt", [P, 512])
        q0 = pb("q0", [P, 512])
        q1 = pb("q1", [P, 512])

        names = """gathers_begun loads_late iota_in idx_src_in idx_dst_in zeroed prep idx_ready prod_done red_done
            silu_done s_ready oh_dve oh_act dist_done w_done scat_done cnt_oh cnt_mm y_mm x_in
            y_copied y_written ys_in y_high y_sub1 y_mid y_sub2 y_out table_written
            w_copied pass_done agg_ready aggn_mm aggn_ready tp_mm tp_prod tp_red
            us_ready us_tr ust_ready upd_mm y_ready mean_mm d_ready sq_ready var_mm std_ready
            rstd_ready ln_ready rows_ln rows_tr x2_ready h_ready h_tr tab_ready rc_chain rcn_tr rct_ready
            scaled x_n_in last_in w_y_in hi_src_ready hi_dst_ready masks_made
            x_mm x_mask_done y_row_mm out_done hi_ready hi_out hi_in cols_made cols_out fetch_mm pick_prod picked
            tab_high tab_sub1 tab_mid parts_ready"""
        S = {n: sem(n) for n in names.split()}
        gathered = [[sem(f"gathered{b}{h}") for h in range(2)] for b in range(2)]
        ea_in = [sem(f"ea_in{b}") for b in range(2)]
        ea0_in = [sem(f"ea0_in{b}") for b in range(2)]
        lo_in = [sem(f"lo_in{b}") for b in range(2)]
        cols_in = [sem(f"cols_in{b}") for b in range(2)]

        block = ctx.enter_context(nc.Block())
        late = (
            (ident[:], ident_d), (avg[:], avg_d), (bdm[:], bd_msg), (bdu[:], bd_upd), (bdt[:], bd_tp),
            (bdr[:, 0, :], bd_root[0]), (bdr[:, 1, :], bd_root[1]), (bdr[:, 2, :], bd_root[2]),
            (br[:], bias_root), (wsel[:], w_sel), (wraw[:, 0:FF], w_rep[0]),
            (wraw[:, FF:2 * FF], w_rep[1]), (wraw[:, 2 * FF:3 * FF], w_rep[2]),
        )
        LATE = 16 * len(late)

        @block.sync
        def _(sp):
            def store_parts(parts, high, mid, low, k, width, done):
                rows = parts.shape[0] // 6
                for n, part in enumerate((high, high, high, mid, mid, low)):
                    view = parts[n * rows:(n + 1) * rows, :].rearrange("i (q c) -> (i q) c", q=P // rows)
                    sp.dma_start(view[:, bass.ds(k * width, width)], part).then_inc(done, 16)

            sp.sem_inc(S["y_out"], 96)
            sp.sem_inc(S["cols_out"], 16)
            sp.dma_start(x0_t[:], x_t).then_inc(S["x_in"], 16)
            sp.dma_start(bdy[:], bd_y_d).then_inc(S["x_in"], 16)
            sp.dma_start(last_i[:], last_d).then_inc(S["last_in"], 16)
            sp.dma_start(column_of[:], column_d).then_inc(S["last_in"], 16)
            sp.dma_start(tab_n[:], x_n).then_inc(S["x_n_in"], 16)
            sp.dma_start(w_y[:], w_y_d).then_inc(S["w_y_in"], 16)
            hi_line = hi_rows.rearrange("r t k e -> (r t k e)").unsqueeze(0)
            lo_line = lo_rows.rearrange("r t e -> (r t e)").unsqueeze(0)
            sp.wait_ge(S["hi_ready"], 1)
            sp.dma_start(hi_rows, last_hi[:]).then_inc(S["hi_out"], 16)
            sp.dma_start(lo_rows, last_lo[:]).then_inc(S["hi_out"], 16)

            def load_hi(i):
                w = SLOTS * 2 * P
                sp.dma_start(hi_all[:].rearrange("p t k e -> p (t k e)"),
                             hi_line[:, bass.ds(i * w, w)].broadcast_to([QUARTER, w])).then_inc(S["hi_in"], 16)

            def load_lo(i, b):
                w = N_FETCH[b] * P
                sp.dma_start(lo_all[:, SLOT[b]:SLOT[b] + N_FETCH[b], :].rearrange("p t e -> p (t e)"),
                             lo_line[:, bass.ds(i * SLOTS * P + SLOT[b] * P, w)].broadcast_to([P, w])).then_inc(lo_in[b], 16)

            def store_columns(i):
                sp.wait_ge(S["cols_made"], i + 1)
                w = SLOTS * 4 * P
                sp.dma_start(columns[:, bass.ds(i * w, w)], cols_new[:, 0].rearrange("p t c e -> p (t c e)")
                             ).then_inc(S["cols_out"], 16)

            sp.wait_ge(S["hi_out"], 32)
            load_hi(0)
            for b in range(2):
                load_lo(0, b)
            store_columns(0)
            sp.dma_start(ys[:], ea1[:, 0:CH1]).then_inc(S["ys_in"], 16)
            for dst, src in late:
                sp.dma_start(dst, src).then_inc(S["loads_late"], 16)

            with sp.Fori(0, ROUNDS) as i:
                sp.wait_ge(S["cols_made"], i + 1)
                load_hi(i + 1)
                for b in range(2):
                    sp.wait_ge(S["prod_done"], upto(i * 2 + b, 2, 0) - 2)
                    sp.dma_start(ea0_now[:, b, :], ea0[:, bass.ds((i * 2 + b) * (G * F_EDGE0), G * F_EDGE0)]
                                 ).then_inc(ea0_in[b], 16)
                    sp.wait_ge(S["x_mask_done"], upto(i * 2 + b, 1, 1))
                    load_lo(i + 1, b)
                store_columns(i + 1)
                sp.wait_ge(S["y_sub2"], i + 1)
                store_parts(parts1, yh[:], ym[:], yl[:], i, CH1, S["y_out"])
                sp.dma_start(ys[:], ea1[:, bass.ds(i * CH1 + CH1, CH1)]).then_inc(S["ys_in"], 16)
            sp.wait_ge(S["y_out"], 96 * ROUNDS + 96)
            sp.wait_ge(S["cols_out"], 16 * ROUNDS + 32)
            sp.wait_ge(S["ys_in"], 16 * ROUNDS + 16)
            sp.wait_ge(S["hi_in"], 16 * ROUNDS + 16)
            for b in range(2):
                sp.wait_ge(lo_in[b], 16 * ROUNDS + 16)
            with sp.Fori(0, LAYERS) as l:
                with sp.Fori(0, ROUNDS) as i:
                    for b in range(2):
                        sp.wait_ge(S["w_done"], upto(l * GROUPS + i * 2 + b, 2, 0) - 2)
                        sp.dma_start(ea[0:ROWS, b, :], parts1[:, bass.ds((i * 2 + b) * (G * P), G * P)]).then_inc(ea_in[b], 16)
                        sp.wait_ge(S["fetch_mm"], upto(l * GROUPS + i * 2 + b, 1, 0) - 1)
                        sp.dma_start(cols_now[:, SLOT[b]:SLOT[b] + N_FETCH[b]].rearrange("p t c e -> p (t c e)"),
                                     columns[:, bass.ds(i * (SLOTS * 4 * P) + SLOT[b] * 4 * P, N_FETCH[b] * 4 * P)]
                                     ).then_inc(cols_in[b], 16)
                sp.wait_ge(S["tab_ready"], l + 2)
                sp.dma_start(table.rearrange("(p n) f -> p (n f)", n=32), tab_n[:]).then_inc(S["table_written"], 16)
            sp.wait_ge(S["ln_ready"], 1)
            sp.dma_start(out, out_t[:]).then_inc(S["out_done"], 16)
            sp.wait_ge(S["table_written"], 16 * (LAYERS + 1))
            sp.wait_ge(S["out_done"], 16)

        @block.gpsimd
        def _(pool):
            def gather_group(rows, to, width, g, turn, b):
                for h in range(2):
                    if h == 0:
                        pool.wait_ge(S["idx_ready"], turn)
                    pool.wait_ge(S["prod_done"], upto(g, 2, h + 1) - 4)
                    pool.sem_inc(S["gathers_begun"], 1)
                    for t in range(h * HALF, min((h + 1) * HALF, FETCH_FROM[b])):
                        pool.indirect_dma_start(
                            out=to[:, b, t * width:(t + 1) * width], out_offset=None, in_=rows,
                            in_offset=bass.IndirectOffsetOnAxis(ap=idx_now[:, b, t:t + 1], axis=0),
                        ).then_inc(gathered[b][h], 16)

            pool.dma_start(iota[:], iota_d).then_inc(S["iota_in"], 16)
            pool.dma_start(idx["src"][:], src_i).then_inc(S["idx_src_in"], 16)
            pool.dma_start(idx["dst"][:], dst_i).then_inc(S["idx_dst_in"], 16)
            pool.wait_ge(S["y_written"], 64)
            with pool.Fori(0, ROUNDS) as i:
                for b in range(2):
                    gather_group(y_table, yg, ROW_Y, i * 2 + b, i * 2 + (b + 1), b)
            with pool.Fori(0, LAYERS) as l:
                with pool.Fori(0, ROUNDS) as i:
                    pool.wait_ge(S["table_written"], l * 16 + 16)
                    for b in range(2):
                        gather_group(table, xg, F, l * GROUPS + i * 2 + (GROUPS + b),
                                     l * (GROUPS + 2) + i * 2 + (GROUPS + 2 + b + 1), b)

        @block.vector
        def _(dve):
            for n, k in (("prod_done", 4), ("red_done", 4), ("s_ready", 4), ("oh_dve", 2), ("cnt_oh", 2), ("picked", 2),
                         ("x_mask_done", 2)):
                dve.sem_inc(S[n], k)
            nc.vector.memset(zeros[:], 0.0)
            nc.vector.memset(eps[:], EPS)
            nc.vector.memset(ea[96:KROWS, :, :], 1.0).then_inc(S["zeroed"], 1)
            made = [0]

            def link(ins):
                made[0] += 1
                ins.then_inc(S["prep"], 1)
                dve.wait_ge(S["prep"], made[0])

            def split_weights():
                link(nc.vector.tensor_copy(whi[:], wraw[:]))
                link(nc.vector.tensor_tensor(wraw[:], wraw[:], whi[:], ALU.subtract))
                link(nc.vector.tensor_copy(wmid[:], wraw[:]))
                link(nc.vector.tensor_tensor(wlow[:], wraw[:], wmid[:], ALU.subtract))
                link(nc.vector.tensor_scalar(wpart[:], whi[:], wsel[:, 0:1], None, ALU.mult))
                for part, j in ((wmid, 1), (wlow, 2)):
                    link(nc.vector.scalar_tensor_tensor(out=wpart[:], in0=part[:], scalar=wsel[:, j:j + 1],
                                                        in1=wpart[:], op0=ALU.mult, op1=ALU.add))

            def table_parts(n):
                dve.wait_ge(S["tab_high"], n)
                nc.vector.tensor_tensor(tab_rest[:], tab_n[:], tab_parts[:, 0, :], ALU.subtract).then_inc(S["tab_sub1"], 1)
                dve.wait_ge(S["tab_mid"], n)
                nc.vector.tensor_tensor(tab_parts[:, 2, :], tab_rest[:], tab_parts[:, 1, :], ALU.subtract
                                        ).then_inc(S["parts_ready"], 1)

            dve.wait_ge(S["last_in"], 32)
            link(nc.vector.tensor_scalar(last_tmp, last_i[:], 3, None, ALU.arith_shift_right))
            link(nc.vector.tensor_copy(last_hi[:], last_tmp))
            link(nc.vector.tensor_scalar(last_tmp[:, :, 1, :], last_i[:, :, 1, :], LO - 1, None, ALU.bitwise_and))
            link(nc.vector.tensor_copy(last_lo[:], last_tmp[:, :, 1, :]))
            dve.sem_inc(S["hi_ready"], 1)

            def make_columns(i):
                dve.wait_ge(S["hi_in"], i * 16 + 16)
                dve.wait_ge(S["cols_out"], i * 16 + 16)
                dve.wait_ge(S["x_mm"], i * 2 + 2)
                for c in range(4):
                    ins = nc.vector.tensor_scalar(cols_new[:, :, :, c, :], hi_all[:].rearrange("p t k e -> p k t e"),
                                                  column_of[0:QUARTER, c:c + 1], None, ALU.is_equal)
                ins.then_inc(S["cols_made"], 1)

            def mask_x(g, u, b):
                dve.wait_ge(S["x_mm"], upto(g, 1, 1))
                dve.wait_ge(lo_in[b], u * 16 + 16)
                dve.wait_ge(S["y_row_mm"], upto(g, 1, 0) - 1)
                s0, s1 = SLOT[b], SLOT[b] + N_FETCH[b]
                nc.vector.scalar_tensor_tensor(
                    out=x_masked[:, s0:s1, :], in0=lo_all[:, s0:s1, :], scalar=column_of[:, 4:5],
                    in1=w_ps[0][:, b * 512:b * 512 + N_FETCH[b] * P].rearrange("p (t e) -> p t e", e=P),
                    op0=ALU.is_equal, op1=ALU.mult).then_inc(S["x_mask_done"], 1)

            def split_hi(k):
                link(nc.vector.tensor_scalar(tmp_i[:], idx[k][:, 0:TILES], 3, None, ALU.arith_shift_right))
                link(nc.vector.tensor_copy(hi_f[k][:], tmp_i[:]))
                link(nc.vector.tensor_scalar(neg_hi[k][:], hi_f[k][:], -1.0, None, ALU.mult))

            dve.wait_ge(S["idx_src_in"], 16)
            split_hi("src")
            dve.sem_inc(S["hi_src_ready"], 1)
            make_columns(0)
            dve.wait_ge(S["x_n_in"], 16)
            table_parts(1)
            nc.vector.tensor_tensor(x2_n[:], tab_n[:], tab_n[:], ALU.add).then_inc(S["x2_ready"], 1)
            dve.wait_ge(S["idx_dst_in"], 16)
            dve.wait_ge(S["iota_in"], 16)
            for n, k in enumerate(KINDS):
                link(nc.vector.tensor_scalar(tmp_i[:], idx[k][:, 0:TILES], LO - 1, None, ALU.bitwise_and))
                link(nc.vector.tensor_copy(lo_f[:, n, :], tmp_i[:]))
            link(nc.vector.tensor_scalar(tmp_i[:], idx["dst"][:, 0:TILES], 5, None, ALU.arith_shift_right))
            link(nc.vector.tensor_copy(row_f[:], tmp_i[:]))
            link(nc.vector.tensor_scalar(tmp_i[:], idx["dst"][:, 0:TILES], 31, None, ALU.bitwise_and))
            link(nc.vector.tensor_copy(col_f[:], tmp_i[:]))

            mask_x(0, 0, 0)

            def products(g, u, b, h):
                dve.wait_ge(gathered[b][h], gathers_done(u, b, h))
                if h == 1:
                    dve.wait_ge(S["picked"], upto(g - GROUPS, 1, 1))
                dve.wait_ge(S["w_done"], upto(g - GROUPS, 2, h + 1))
                dve.wait_ge(S["red_done"], upto(g, 2, h + 1) - 2)
                nc.vector.scalar_tensor_tensor(
                    out=prod[:, h, :].rearrange("p (i o) -> p i o", o=F), in0=w_ps[h][:].rearrange("p (i o) -> p i o", o=F),
                    scalar=0.0, in1=xg[:, b, h * HALF * F:(h + 1) * HALF * F].unsqueeze(2).broadcast_to([P, HALF * F, F]),
                    op0=ALU.max, op1=ALU.mult).then_inc(S["prod_done"], 1)

            def first_products(g, u, b, h):
                dve.wait_ge(gathered[b][h], gathers_done(u, b, h))
                dve.wait_ge(ea0_in[b], u * 16 + 16)
                dve.wait_ge(S["red_done"], upto(g, 2, h + 1) - 2)

                def multiply(rows, first, last):
                    w = (last - first) * F_EDGE0
                    at = (first - h * HALF) * ROW_Y
                    return nc.vector.tensor_tensor(
                        prod[:, h, at:at + w * F].rearrange("p (j o) -> p j o", o=F), rows.rearrange("p (j o) -> p j o", o=F),
                        ea0_now[:, b, first * F_EDGE0:last * F_EDGE0].unsqueeze(2).broadcast_to([P, w, F]), ALU.mult)

                end = min((h + 1) * HALF, FETCH_FROM[b])
                ins = multiply(yg[:, b, h * HALF * ROW_Y:end * ROW_Y], h * HALF, end)
                if h == 1:
                    dve.wait_ge(S["y_row_mm"], upto(g, 1, 1))
                    ins = multiply(w_ps[1][:, b * 512:b * 512 + N_FETCH[b] * ROW_Y], end, G)
                ins.then_inc(S["prod_done"], 1)

            def reduce_half(g, b, h, free, inner):
                dve.wait_ge(S["prod_done"], upto(g, 2, h + 1))
                dve.wait_ge(free, upto(g, 2, h + 1) - 4)
                nc.vector.tensor_reduce(
                    out=msg[:, b, h * HALF * F:(h + 1) * HALF * F].rearrange("p (t o) -> p t o", o=F),
                    in_=prod[:, h, 0:HALF * inner * F].rearrange("p (t i o) -> p t o i", i=inner, o=F), axis=AX.X, op=ALU.add,
                ).then_inc(S["red_done"], 1)

            def one_hots(g, local, b, which, tiles):
                dve.wait_ge(S["scat_done"], upto(g, 1, 0) - 1)
                for t in tiles:
                    ins = nc.vector.tensor_scalar(onehot[:, b, t, :], iota[:], hi_f[which][:, bass.ds(local * G + t, 1)],
                                                  None, ALU.is_equal)
                ins.then_inc(S["oh_dve"], 1)

            def spread_half(g, local, b, h, which, source, ready):
                dve.wait_ge(ready, upto(g, 2, h + 1))
                nc.vector.tensor_tensor(
                    spread[:, b, h * HALF * P:(h + 1) * HALF * P].rearrange("p (t a o) -> p t a o", a=LO, o=F),
                    mask[which][:, bass.ds(local * (G * LO) + h * HALF * LO, HALF * LO)].rearrange("p (t a) -> p t a", a=LO)
                    .unsqueeze(3).broadcast_to([P, HALF, LO, F]),
                    source[:, b, h * HALF * F:(h + 1) * HALF * F].rearrange("p (t o) -> p t o", o=F)
                    .unsqueeze(2).broadcast_to([P, HALF, LO, F]),
                    ALU.mult).then_inc(S["s_ready"], 1)

            def pick(g, local, b):
                dve.wait_ge(S["fetch_mm"], upto(g - GROUPS, 1, 1))
                dve.wait_ge(S["picked"], upto(g - GROUPS, 1, 0))
                n = N_FETCH[b]
                nc.vector.tensor_tensor(
                    picks[:, 0:n * P].rearrange("p (t a f) -> p t a f", a=LO, f=F),
                    cnt[:, SLOT[b] * P:(SLOT[b] + n) * P].rearrange("p (t a f) -> p t a f", a=LO, f=F),
                    mask["src"][:, bass.ds(local * (G * LO) + FETCH_FROM[b] * LO, n * LO)].rearrange("p (t a) -> p t a", a=LO)
                    .unsqueeze(3).broadcast_to([P, n, LO, F]), ALU.mult).then_inc(S["pick_prod"], 1)

            def sum_picks(g, b):
                dve.wait_ge(S["pick_prod"], g - (GROUPS - 1))
                dve.wait_ge(S["prod_done"], upto(g, 2, 2) - 4)
                nc.vector.tensor_reduce(out=xg[:, b, FETCH_FROM[b] * F:G * F].rearrange("p (t f) -> p t f", f=F),
                                        in_=picks[:, 0:N_FETCH[b] * P].rearrange("p (t a f) -> p t f a", a=LO, f=F),
                                        axis=AX.X, op=ALU.add).then_inc(S["picked"], 1)

            def count_rows(local, to, number, width):
                return nc.vector.tensor_tensor(
                    to[:].rearrange("p (t w) -> p t w", w=width),
                    number[:, bass.ds(local * G, G)].unsqueeze(2).broadcast_to([P, G, width]),
                    iota[:, 0:width].unsqueeze(1).broadcast_to([P, G, width]), ALU.is_equal)

            def group(g, u, local, b, which, first_pass):
                free = S["silu_done"] if first_pass else S["s_ready"]
                inner = F_EDGE0 if first_pass else F
                if first_pass:
                    nc.vector.tensor_tensor(
                        masks[:, :, bass.ds(local * (G * LO), G * LO)].rearrange("p k (t a) -> p k t a", a=LO),
                        lo_f[:, :, bass.ds(local * G, G)].unsqueeze(3).broadcast_to([P, 2, G, LO]),
                        iota[:, 0:LO].unsqueeze(1).unsqueeze(1).broadcast_to([P, 2, G, LO]), ALU.is_equal
                    ).then_inc(S["masks_made"], 1)
                    mask_x(g + 1, u + b, 1 - b)
                    if b == 0:
                        make_columns(u + 1)
                one_hots(g, local, b, which, range(FIRST_ACT_TILE[0 if first_pass else 1]))
                if first_pass and b == 0:
                    dve.wait_ge(S["y_high"], u + 1)
                    nc.vector.tensor_tensor(ys[:], ys[:], yh[:], ALU.subtract).then_inc(S["y_sub1"], 1)
                if first_pass:
                    first_products(g, u, b, 0)
                    first_products(g, u, b, 1)
                    reduce_half(g, b, 0, free, inner)
                    reduce_half(g, b, 1, free, inner)
                else:
                    pick(g, local, b)
                    products(g, u, b, 0)
                    sum_picks(g, b)
                    reduce_half(g, b, 0, free, inner)
                    products(g, u, b, 1)
                    spread_half(g, local, b, 0, which, msg, S["red_done"])
                    reduce_half(g, b, 1, free, inner)
                    spread_half(g, local, b, 1, which, msg, S["red_done"])
                if first_pass:
                    if b == 0:
                        dve.wait_ge(S["y_mid"], u + 1)
                        nc.vector.tensor_tensor(yl[:], ys[:], ym[:], ALU.subtract).then_inc(S["y_sub2"], 1)
                    dve.wait_ge(S["cnt_mm"], g + 1)
                    count_rows(local, crow, row_f, QUARTER)
                    count_rows(local, ccol, col_f, 32).then_inc(S["cnt_oh"], 1)
                    dve.wait_ge(S["masks_made"], g + 1)
                    for h in range(2):
                        spread_half(g, local, b, h, which, act_msg, S["silu_done"])

            dve.wait_ge(S["y_written"], 64)
            with dve.Fori(0, ROUNDS) as i:
                for b in range(2):
                    group(i * 2 + b, i, i * 2 + b, b, "src", True)

            dve.wait_ge(S["loads_late"], LATE)
            split_weights()
            dve.wait_ge(S["pass_done"], 1)
            nc.vector.tensor_scalar(rc_s[:], cnt[0:QUARTER, 0:32], 1.0, None, ALU.max).then_inc(S["rc_chain"], 1)
            dve.wait_ge(S["rc_chain"], 1)
            nc.vector.reciprocal(rc_s[:], rc_s[:]).then_inc(S["rc_chain"], 1)
            dve.wait_ge(S["rc_chain"], 2)
            nc.vector.tensor_copy(rc_n[:].rearrange("p (m f) -> p m f", f=F),
                                  rc_s[:].unsqueeze(2).broadcast_to([QUARTER, 32, F])).then_inc(S["rc_chain"], 1)

            dve.wait_ge(S["aggn_ready"], 1)
            for k in range(8):
                h = k % 2
                dve.wait_ge(S["tp_mm"], k + 1)
                if k >= 2:
                    dve.wait_ge(S["tp_red"], k - 1)
                nc.vector.tensor_tensor(
                    prod[0:QUARTER, h, :].rearrange("p (i o) -> p i o", o=F),
                    w_ps[h][0:QUARTER, :].rearrange("p (i o) -> p i o", o=F),
                    agg_n[:, k * HALF * F:(k + 1) * HALF * F].unsqueeze(2).broadcast_to([QUARTER, HALF * F, F]),
                    ALU.mult).then_inc(S["tp_prod"], 1)
                dve.wait_ge(S["tp_prod"], k + 1)
                nc.vector.tensor_reduce(
                    out=u_n[:, k * HALF * F:(k + 1) * HALF * F].rearrange("p (t o) -> p t o", o=F),
                    in_=prod[0:QUARTER, h, :].rearrange("p (t i o) -> p t o i", i=F, o=F), axis=AX.X,
                    op=ALU.add).then_inc(S["tp_red"], 1)
            def rows(of):
                return of[:].rearrange("p (m f) -> p m f", f=F)

            def over_features(of):
                return of[:].unsqueeze(2).broadcast_to([QUARTER, 32, F])

            dve.wait_ge(S["upd_mm"], 1)
            dve.wait_ge(S["x2_ready"], 1)
            nc.vector.scalar_tensor_tensor(out=v_n[:], in0=q0[0:QUARTER, :], scalar=NORM_LIN, in1=x2_n[:],
                                           op0=ALU.mult, op1=ALU.add).then_inc(S["rows_ln"], 1)
            dve.wait_ge(S["rows_ln"], 1)
            nc.vector.tensor_reduce(out=sum_n[:], in_=rows(v_n), axis=AX.X, op=ALU.add).then_inc(S["rows_ln"], 1)
            dve.wait_ge(S["rows_ln"], 2)
            nc.vector.scalar_tensor_tensor(out=rows(d_n), in0=over_features(sum_n), scalar=-1.0 / F, in1=rows(v_n),
                                           op0=ALU.mult, op1=ALU.add).then_inc(S["rows_ln"], 1)
            dve.wait_ge(S["rows_ln"], 4)
            nc.vector.tensor_reduce(out=sum_n[:], in_=rows(sq_n), axis=AX.X, op=ALU.add).then_inc(S["rows_ln"], 1)
            dve.wait_ge(S["rows_ln"], 6)
            nc.vector.reciprocal(std_n[:], std_n[:]).then_inc(S["rows_ln"], 1)
            dve.wait_ge(S["rows_ln"], 7)
            nc.vector.tensor_tensor(rows(tab_n), rows(d_n), over_features(std_n), ALU.mult).then_inc(S["tab_ready"], 1)
            split_hi("dst")
            dve.sem_inc(S["hi_dst_ready"], 1)

            def layer_norm(to):
                dve.wait_ge(S["mean_mm"], 1)
                nc.vector.tensor_tensor(d_t[:], y_t[:], q0[:, 0:HI], ALU.subtract).then_inc(S["d_ready"], 1)
                dve.wait_ge(S["std_ready"], 1)
                nc.vector.reciprocal(std_t[:], std_t[:]).then_inc(S["rstd_ready"], 1)
                dve.wait_ge(S["rstd_ready"], 1)
                nc.vector.tensor_tensor(to[:], d_t[:], std_t[:], ALU.mult).then_inc(S["ln_ready"], 1)

            with dve.Fori(0, LAYERS) as l:
                table_parts(l + 2)
                with dve.Fori(0, ROUNDS) as i:
                    for b in range(2):
                        group(l * GROUPS + i * 2 + (GROUPS + b), l * ROUNDS + i + ROUNDS, i * 2 + b, b, "dst", False)
                dve.wait_ge(S["rct_ready"], 1)
                dve.wait_ge(S["scat_done"], upto(l * GROUPS + (2 * GROUPS - 1), 1, 1))
                nc.vector.tensor_tensor(y_t[:], acc[:, 0:HI], rc_t[:], ALU.mult).then_inc(S["scaled"], 1)
                dve.wait_ge(S["scaled"], l + 1)
                nc.vector.scalar_tensor_tensor(out=h_t[:], in0=q0[:, 0:HI], scalar=br_now[:], in1=y_t[:],
                                               op0=ALU.add, op1=ALU.add).then_inc(S["h_ready"], 1)
            dve.wait_ge(S["h_ready"], LAYERS + 1)
            nc.vector.tensor_tensor(y_t[:], h_t[:], x1_t[:], ALU.add).then_inc(S["y_ready"], 1)
            layer_norm(out_t)

        @block.scalar
        def _(act):
            for n, k in (("oh_act", 2), ("silu_done", 4)):
                act.sem_inc(S[n], k)

            def copy_indices(which, local, b):
                nc.scalar.activation(idx_now[:, b, :], idx[which][:, bass.ds(local * G, G)], ACT.Copy).then_inc(S["idx_ready"], 1)

            act.wait_ge(S["idx_dst_in"], 16)
            for b in range(2):
                copy_indices("dst", b, b)
            for c in range(4):
                act.wait_ge(S["y_mm"], c + 1)
                rows = y_n[:, c * LO * ROW_Y:(c + 1) * LO * ROW_Y]
                nc.scalar.activation(rows, w_ps[c % 2][0:QUARTER, :], ACT.Copy).then_inc(S["y_copied"], 1)
                act.wait_ge(S["y_copied"], c + 1)
                act.dma_start(y_table.rearrange("(p c a) r -> p c (a r)", c=4, a=LO)[:, c, :], rows).then_inc(S["y_written"], 16)
                if c == 0:
                    act.wait_ge(S["x_n_in"], 16)
                    nc.scalar.activation(tab_parts[:, 0, :], tab_n[:], ACT.Copy).then_inc(S["tab_high"], 1)
            act.wait_ge(S["tab_sub1"], 1)
            nc.scalar.activation(tab_parts[:, 1, :], tab_rest[:], ACT.Copy).then_inc(S["tab_mid"], 1)
            act.wait_ge(S["hi_src_ready"], 1)
            act.wait_ge(S["iota_in"], 16)
            act.wait_ge(S["y_written"], 64)

            def one_hots(g, local, b, which, first, between=None):
                act.wait_ge(S["oh_act"], upto(g, 1, 0))
                for t in range(first, G):
                    ins = nc.scalar.activation(dist[:, t - first, :], iota[:], ACT.Abs,
                                               bias=neg_hi[which][:, bass.ds(local * G + t, 1)])
                ins.then_inc(S["dist_done"], 1)
                if between:
                    between()
                act.wait_ge(S["scat_done"], upto(g, 1, 0) - 1)
                act.wait_ge(S["dist_done"], g + 1)
                nc.scalar.activation(onehot[:, b, first:G, :], dist[:, 0:G - first, :], ACT.Relu, scale=-1.0, bias=1.0
                                     ).then_inc(S["oh_act"], 1)

            def silu_half(g, b, h):
                act.wait_ge(S["red_done"], upto(g, 2, h + 1))
                act.wait_ge(S["s_ready"], upto(g, 2, h + 1) - 4)
                nc.scalar.activation(act_msg[:, b, h * HALF * F:(h + 1) * HALF * F], msg[:, b, h * HALF * F:(h + 1) * HALF * F],
                                     ACT.Silu, scale=NORM_MSG).then_inc(S["silu_done"], 1)

            def next_indices(which, u, local, b):
                for h in range(2):
                    act.wait_ge(gathered[b][h], gathers_done(u, b, h))
                act.wait_ge(S["idx_dst_in"], 16)
                copy_indices(which, local + 2, b)

            with act.Fori(0, ROUNDS) as i:
                for b in range(2):
                    between = None
                    if b == 0:
                        act.wait_ge(S["ys_in"], i * 16 + 16)
                        act.wait_ge(S["y_out"], i * 96 + 96)
                        nc.scalar.activation(yh[:], ys[:], ACT.Copy).then_inc(S["y_high"], 1)

                        def between():
                            act.wait_ge(S["y_sub1"], i + 1)
                            nc.scalar.activation(ym[:], ys[:], ACT.Copy).then_inc(S["y_mid"], 1)

                    one_hots(i * 2 + b, i * 2 + b, b, "src", FIRST_ACT_TILE[0], between)
                    next_indices("dst", i, i * 2 + b, b)
                    for h in range(2):
                        silu_half(i * 2 + b, b, h)

            act.wait_ge(S["pass_done"], 1)
            nc.scalar.activation(agg_t[:], acc[:, 0:HI], ACT.Copy).then_inc(S["agg_ready"], 1)
            act.wait_ge(S["aggn_mm"], 1)
            nc.scalar.activation(agg_n[:], q1[0:QUARTER, :], ACT.Copy, scale=NORM_LIN).then_inc(S["aggn_ready"], 1)
            act.wait_ge(S["rcn_tr"], 1)
            nc.scalar.activation(rc_t[:].rearrange("q (p c) -> q c p", c=4),
                                 q0[:, 0:HI].rearrange("q (c p) -> q c p", c=4), ACT.Copy).then_inc(S["rct_ready"], 1)
            act.wait_ge(S["tp_red"], 8)
            nc.scalar.activation(us_n[:], u_n[:], ACT.Silu, scale=NORM_UPD).then_inc(S["us_ready"], 1)
            act.wait_ge(S["us_tr"], 1)
            nc.scalar.activation(us_t[:], q1[:, 0:HI], ACT.Copy).then_inc(S["ust_ready"], 1)
            act.wait_ge(S["rows_ln"], 3)
            nc.scalar.activation(sq_n[:], d_n[:], ACT.Square).then_inc(S["rows_ln"], 1)
            act.wait_ge(S["rows_ln"], 5)
            nc.scalar.activation(std_n[:], sum_n[:], ACT.Sqrt, scale=1.0 / F, bias=eps[0:QUARTER]).then_inc(S["rows_ln"], 1)

            def layer_norm():
                act.wait_ge(S["d_ready"], 1)
                nc.scalar.activation(sq_t[:], d_t[:], ACT.Square).then_inc(S["sq_ready"], 1)
                act.wait_ge(S["var_mm"], 1)
                nc.scalar.activation(std_t[:], q1[:, 0:HI], ACT.Sqrt, bias=eps[:]).then_inc(S["std_ready"], 1)

            act.wait_ge(S["tab_ready"], 1)
            act.dma_start(table.rearrange("(p n) f -> p (n f)", n=32), tab_n[:]).then_inc(S["table_written"], 16)

            act.wait_ge(S["rows_tr"], 1)
            for to in (x1_t, h_t):
                ins = nc.scalar.activation(to[:].rearrange("q (p c) -> q c p", c=4),
                                           q1[:, 0:HI].rearrange("q (c p) -> q c p", c=4), ACT.Copy)
            ins.then_inc(S["h_ready"], 1)

            act.wait_ge(S["hi_dst_ready"], 1)
            with act.Fori(0, LAYERS) as l:
                act.wait_ge(S["idx_ready"], l * (GROUPS + 2) + (GROUPS + 2))
                for b in range(2):
                    copy_indices("src", b, b)
                act.wait_ge(S["tab_ready"], l + 1)
                act.wait_ge(S["x_mm"], GROUPS + 4)
                nc.scalar.activation(tab_parts[:, 0, :], tab_n[:], ACT.Copy).then_inc(S["tab_high"], 1)
                act.wait_ge(S["h_ready"], l + 1)
                nc.scalar.activation(w_now[:], wpart[:, bass.ds(l * FF, FF)], ACT.Copy)
                nc.scalar.activation(bdr_now[:], bdr[:].rearrange("p l c -> p (l c)")[:, bass.ds(l * P, P)], ACT.Copy)
                nc.scalar.activation(br_now[:], br[:, bass.ds(l, 1)], ACT.Copy).then_inc(S["w_copied"], 1)
                act.wait_ge(S["tab_sub1"], l + 2)
                nc.scalar.activation(tab_parts[:, 1, :], tab_rest[:], ACT.Copy).then_inc(S["tab_mid"], 1)
                with act.Fori(0, ROUNDS) as i:
                    for b in range(2):
                        one_hots(l * GROUPS + i * 2 + (GROUPS + b), i * 2 + b, b, "dst", FIRST_ACT_TILE[1])
                        next_indices("src", l * ROUNDS + i + ROUNDS, i * 2 + b, b)
                act.wait_ge(S["h_tr"], l + 1)
                act.wait_ge(S["table_written"], l * 16 + 16)
                nc.scalar.activation(tab_n[:], q1[0:QUARTER, :], ACT.Copy).then_inc(S["tab_ready"], 1)
            layer_norm()

        @block.tensor
        def _(pe):
            for n, k in (("w_done", 4), ("scat_done", 2), ("cnt_mm", 1), ("fetch_mm", 2), ("x_mm", 2), ("y_row_mm", 2)):
                pe.sem_inc(S[n], k)
            x_view = x0_t[:].rearrange("q (p c) -> q c p", c=4)

            pe.wait_ge(S["x_in"], 32)
            for c in range(4):
                if c >= 2:
                    pe.wait_ge(S["y_copied"], c - 1)
                for j in range(2):
                    last = nc.tensor.matmul(w_ps[c % 2][0:QUARTER, j * 512:(j + 1) * 512], x_view[:, c, :],
                                            bdy[:, j * 512:(j + 1) * 512], start=True, stop=True)
                last.then_inc(S["y_mm"], 1)

            def weights(g, u, b):
                pe.wait_ge(ea_in[b], (u - ROUNDS) * 16 + 16)
                for h in range(2):
                    pe.wait_ge(S["prod_done"], upto(g, 2, h + 1) - 2)
                    for j in range(HALF):
                        t = h * HALF + j
                        last = nc.tensor.matmul(w_ps[h][:, j * FF:(j + 1) * FF], ea[:, b, t * P:(t + 1) * P],
                                                w_now[:], start=True, stop=True)
                    last.then_inc(S["w_done"], 1)

            def fetch(g, u, b):
                pe.wait_ge(cols_in[b], (u - ROUNDS) * 16 + 16)
                pe.wait_ge(S["picked"], upto(g - GROUPS, 1, 0) - 1)
                for t in range(SLOT[b], SLOT[b] + N_FETCH[b]):
                    for c in range(4):
                        for part in range(3):
                            last = nc.tensor.matmul(cnt[:, t * P:(t + 1) * P], cols_now[:, t, c, :],
                                                    tab_parts[:, part, c * P:(c + 1) * P], start=c + part == 0,
                                                    stop=c + part == 5)
                last.then_inc(S["fetch_mm"], 1)

            def prepare(g, u, b):
                weights(g, u, b)
                fetch(g, u, b)

            def fetch_x(g, u, b):
                s0, s1 = SLOT[b], SLOT[b] + N_FETCH[b]
                pe.wait_ge(S["cols_made"], u + 1)
                pe.wait_ge(S["x_mask_done"], upto(g, 1, 0) - 1)
                for c in range(4):
                    for part in range(3):
                        last = nc.tensor.matmul(w_ps[0][:, b * 512:b * 512 + N_FETCH[b] * P],
                                                tab_parts[:, part, c * P:(c + 1) * P], cols_new[:, 1, s0:s1, c, :],
                                                start=c + part == 0, stop=c + part == 5)
                last.then_inc(S["x_mm"], 1)

            def y_row(g, b):
                pe.wait_ge(S["x_mask_done"], upto(g, 1, 1))
                pe.wait_ge(S["prod_done"], upto(g, 2, 0) - 2)
                for t in range(N_FETCH[b]):
                    at = b * 512 + t * ROW_Y
                    last = nc.tensor.matmul(w_ps[1][:, at:at + ROW_Y], x_masked[:, SLOT[b] + t, :], w_y[:], start=True,
                                            stop=True)
                last.then_inc(S["y_row_mm"], 1)

            def scatter(g, b, counts, end=False):
                if counts:
                    pe.wait_ge(S["cnt_oh"], upto(g, 1, 1))
                    for t in range(G):
                        last = nc.tensor.matmul(cnt[0:QUARTER, 0:32], crow[:, t * QUARTER:(t + 1) * QUARTER],
                                                ccol[:, t * 32:(t + 1) * 32], start=False, stop=False)
                    last.then_inc(S["cnt_mm"], 1)
                pe.wait_ge(S["oh_dve"], upto(g, 1, 1))
                pe.wait_ge(S["oh_act"], upto(g, 1, 1))
                for h in range(2):
                    pe.wait_ge(S["s_ready"], upto(g, 2, h + 1))
                    for t in range(h * HALF, (h + 1) * HALF):
                        last = nc.tensor.matmul(acc[:, 0:HI], spread[:, b, t * P:(t + 1) * P], onehot[:, b, t, :],
                                                start=False, stop=end and t == G - 1)
                last.then_inc(S["scat_done"], 1)

            def clear(to, start):
                return nc.tensor.matmul(to, zeros[:, 0:to.shape[0]], zeros[:, 0:to.shape[1]], start=start, stop=not start)

            def first_pass():
                clear(acc[:, 0:HI], True)
                clear(cnt[0:QUARTER, 0:32], True)
                for b in range(2):
                    fetch_x(b, 0, b)
                y_row(0, 0)
                with pe.Fori(0, ROUNDS) as i:
                    for b in range(2):
                        fetch_x(i * 2 + (b + 2), i + 1, b)
                        y_row(i * 2 + (b + 1), 1 - b)
                        scatter(i * 2 + b, b, True)
                clear(cnt[0:QUARTER, 0:32], False)
                clear(acc[:, 0:HI], False).then_inc(S["pass_done"], 1)

            def edge_pass(g0, u0):
                clear(acc[:, 0:HI], True)
                prepare(g0, u0, 0)
                with pe.Fori(0, ROUNDS - 1) as i:
                    prepare(i * 2 + g0 + 1, i + u0, 1)
                    scatter(i * 2 + g0, 0, False)
                    prepare(i * 2 + g0 + 2, i + u0 + 1, 0)
                    scatter(i * 2 + g0 + 1, 1, False)
                prepare(g0 + (GROUPS - 1), u0 + (ROUNDS - 1), 1)
                scatter(g0 + (GROUPS - 2), 0, False)
                nc.tensor.matmul(q0[:, 0:HI], bdr_now[:], h_t[:], start=True, stop=True)
                scatter(g0 + (GROUPS - 1), 1, False, end=True)

            def to_rows(of, done):
                view = of[:].rearrange("q (p c) -> q c p", c=4)
                for c in range(4):
                    last = nc.tensor.transpose(q1[0:QUARTER, c * P:(c + 1) * P], view[:, c, :], ident[:])
                last.then_inc(done, 1)

            def to_columns(to, of, done):
                for c in range(4):
                    last = nc.tensor.transpose(to[:, c * QUARTER:(c + 1) * QUARTER], of[:, c * P:(c + 1) * P],
                                               ident[0:QUARTER, 0:QUARTER])
                last.then_inc(done, 1)

            def layer_norm():
                pe.wait_ge(S["y_ready"], 1)
                nc.tensor.matmul(q0[:, 0:HI], avg[:], y_t[:], start=True, stop=True).then_inc(S["mean_mm"], 1)
                pe.wait_ge(S["sq_ready"], 1)
                nc.tensor.matmul(q1[:, 0:HI], avg[:], sq_t[:], start=True, stop=True).then_inc(S["var_mm"], 1)

            def transform(k):
                h = k % 2
                if k >= 2:
                    pe.wait_ge(S["tp_prod"], k - 1)
                for j in range(2):
                    at = h * HALF * FF + j * 512
                    last = nc.tensor.matmul(w_ps[h][0:QUARTER, j * 512:(j + 1) * 512], x_view[:, k // 2, :],
                                            bdt[:, at:at + 512], start=True, stop=True)
                last.then_inc(S["tp_mm"], 1)

            pe.wait_ge(S["zeroed"], 1)
            pe.wait_ge(S["w_y_in"], 16)
            pe.wait_ge(S["y_copied"], 4)
            pe.wait_ge(S["parts_ready"], 1)
            first_pass()
            pe.wait_ge(S["loads_late"], LATE)
            pe.wait_ge(S["prod_done"], upto(GROUPS - 1, 2, 2))
            transform(0)
            transform(1)
            pe.wait_ge(S["agg_ready"], 1)
            agg_view = agg_t[:].rearrange("q (p c) -> q c p", c=4)
            for c in range(4):
                last = nc.tensor.matmul(q1[0:QUARTER, c * P:(c + 1) * P], agg_view[:, c, :], bdm[:], start=True, stop=True)
            last.then_inc(S["aggn_mm"], 1)
            for k in range(2, 8):
                transform(k)
            pe.wait_ge(S["rc_chain"], 3)
            to_columns(q0, rc_n, S["rcn_tr"])
            pe.wait_ge(S["us_ready"], 1)
            to_columns(q1, us_n, S["us_tr"])
            pe.wait_ge(S["ust_ready"], 1)
            pe.wait_ge(S["rct_ready"], 1)
            for c in range(4):
                last = nc.tensor.matmul(q0[0:QUARTER, c * P:(c + 1) * P], us_t[:, c * QUARTER:(c + 1) * QUARTER], bdu[:],
                                        start=True, stop=True)
            last.then_inc(S["upd_mm"], 1)
            pe.wait_ge(S["tab_ready"], 1)
            to_columns(q1, tab_n, S["rows_tr"])

            with pe.Fori(0, LAYERS) as l:
                pe.wait_ge(S["w_copied"], l + 1)
                pe.wait_ge(S["parts_ready"], l + 2)
                edge_pass(l * GROUPS + GROUPS, l * ROUNDS + ROUNDS)
                pe.wait_ge(S["h_ready"], l + 2)
                to_rows(h_t, S["h_tr"])
            pe.wait_ge(S["tab_ready"], LAYERS + 1)
            layer_norm()


def kernel(**inputs):
    import numpy as np
    import concourse.bacc as bacc
    from concourse.bass_utils import run_bass_kernel_spmd as run

    a = {k: np.asarray(v) for k, v in inputs.items()}
    f4 = np.float32

    def blocks(w):
        o = np.zeros((P, LO * w.shape[1]), w.dtype)
        for k in range(LO):
            o[k * F:(k + 1) * F, k * w.shape[1]:(k + 1) * w.shape[1]] = w
        return o

    def rows(w, bias):
        o = np.zeros((KROWS, FF), w.dtype)
        for k in range(6):
            o[k * w.shape[0]:(k + 1) * w.shape[0]] = w
        o[96:99] = bias
        return o

    def select():
        o = np.zeros((KROWS, 3), f4)
        for k, part in enumerate((0, 1, 2, 0, 1, 0)):
            o[k * F:(k + 1) * F, part] = 1.0
        o[96:99] = np.eye(3, dtype=f4)
        return o

    def indices(v):
        o = np.full(EDGES + 2 * G * P, PAD_NODE, np.int32)
        o[:N_EDGES] = v
        return np.ascontiguousarray(o.reshape(TILES + 2 * G, P).T)

    def by_edge(v):
        o = np.zeros((EDGES, v.shape[1]), v.dtype)
        o[:N_EDGES] = v
        return o.reshape(TILES, P, -1).transpose(1, 0, 2).reshape(P, -1)

    def flat(v):
        o = np.zeros((v.shape[1], EDGES), v.dtype)
        o[:, :N_EDGES] = v.T
        o = o.reshape(P, -1)
        return np.concatenate([o, np.zeros((P, CH1), v.dtype)], 1)

    x = np.zeros((NODES, F), a["x"].dtype)
    x[:N_NODES] = a["x"]
    upd = a["L0_gnn_W_upd_tp"].reshape(F, FF)
    layers = ("1", "2", "3")
    fetched = [b * G + t for b in range(2) for t in range(FETCH_FROM[b], G)]
    column = np.zeros((P, 5), f4)
    column[:QUARTER, 0:4] = np.arange(HI).reshape(QUARTER, 4)
    column[:, 4] = np.arange(P) // F
    arrays = {
        "x_t": np.ascontiguousarray(x.reshape(HI, LO * F).T),
        "src": indices(a["src"]), "dst": indices(a["dst"]),
        "ea0": by_edge(a["edge_attr_8"]), "ea1": flat(a["edge_attr_16"]),
        "bd_y": blocks(a["L0_gnn_W_msg_tp"].reshape(F, ROW_Y)),
        "w": np.stack([rows(a[f"L1_gnn_Wn{k}"], a[f"L1_gnn_bn{k}"]) for k in layers]),
        "sel": select(),
        "bd_msg": blocks(a["L0_gnn_W_msg_lin"]), "bd_upd": blocks(a["L0_gnn_W_upd_lin"]),
        "bd_root": np.stack([blocks(a[f"L1_gnn_Wr{k}"]) for k in layers]),
        "bias_root": np.ascontiguousarray(np.stack([np.tile(a[f"L1_gnn_b{k}"], LO) for k in layers]).T),
        "bd_tp": blocks(upd),
        "ident": np.eye(P, dtype=f4),
        "iota": np.tile(np.arange(HI, dtype=f4), (P, 1)),
        "avg": np.kron(np.eye(LO, dtype=f4), np.full((F, F), 1.0 / F, f4)),
        "last": np.stack([indices(a[k]).T.reshape(ROUNDS + 1, 2 * G, P)[:, fetched] for k in ("src", "dst")], 2),
        "column": column,
        "x_n": x.reshape(QUARTER, 4 * P),
        "w_y": np.tile(a["L0_gnn_W_msg_tp"].reshape(F, ROW_Y), (LO, 1)),
    }
    arrays = {f"in_{k}": np.ascontiguousarray(v) for k, v in arrays.items()}
    nc = bacc.Bacc("TRN2", target_bir_lowering=False, num_devices=1)
    args = [nc.dram_tensor(k, v.shape, mybir.dt.from_np(v.dtype), kind="ExternalInput").ap() for k, v in arrays.items()]
    out = nc.dram_tensor("out_nodes", (P, HI), mybir.dt.float32, kind="ExternalOutput").ap()
    gnn_kernel(nc, *args, out)
    got = run(nc, [arrays], core_ids=[0]).results[0]["out_nodes"]
    return np.ascontiguousarray(got.T.reshape(NODES, F)[:N_NODES])
```
